# Optimizing a Trainium2 kernel written in Bass

```python
import numpy as np
import jax
import jax.numpy as jnp

def _softmax(x, axis=-1):
    return jax.nn.softmax(x, axis=axis)

def _gelu(x):
    return jax.nn.gelu(x, approximate=True)

def _silu(x):
    return jax.nn.silu(x)

def _sigmoid(x):
    return jax.nn.sigmoid(x)

def _layernorm(x, axis=-1, eps=1e-05):
    m = jnp.mean(x, axis=axis, keepdims=True)
    v = jnp.var(x, axis=axis, keepdims=True)
    return (x - m) / jnp.sqrt(v + eps)

def _scatter_add(tgt, idx, src, axis=0):
    return tgt.at[idx].add(src)

def _segment_sum(src, seg, n):
    return jax.ops.segment_sum(src, seg, n)
kernel_name = 'mk_conv_seq_d2_conv_nhwc256_r4_a34858'

def setup_inputs(seed: int=0):
    np.random.seed(seed)
    _w = jnp.asarray

    def _rec_inputs():
        import jax
        import jax.numpy as jnp
        _gk = jax.random.key(seed)
        x = -0.0003929 + 0.9999 * jax.random.normal(jax.random.fold_in(_gk, 1), (16, 16, 16, 64), jnp.float32)
        return x
    x = _rec_inputs()

    def _L0_conv_setup():
        import jax, jax.numpy as jnp
        import numpy as np

        def _maxpool2x2(t):
            B, H, W, C = t.shape
            return t.reshape(B, H // 2, 2, W // 2, 2, C).max(axis=(2, 4))
        key = jax.random.key(seed)
        ks = jax.random.split(key, 7)
        B, H, W, C = (16, 16, 16, 64)
        x = jax.random.normal(ks[0], (B, H, W, C), jnp.float32)
        w_theta = jax.random.normal(ks[1], (C, C // 8), jnp.float32) * 0.05
        w_phi = jax.random.normal(ks[2], (C, C // 8), jnp.float32) * 0.05
        w_g = jax.random.normal(ks[3], (C, C // 2), jnp.float32) * 0.05
        w_o = jax.random.normal(ks[4], (C // 2, C), jnp.float32) * 0.05
        b_o = jnp.zeros((C,), jnp.float32)
        sigma = jax.random.normal(ks[5], (), jnp.float32)
        return {'x': x, 'w_theta': w_theta, 'w_phi': w_phi, 'w_g': w_g, 'w_o': w_o, 'b_o': b_o, 'sigma': sigma}
    _L0_conv_all = _L0_conv_setup()
    _L0_conv_in = {k: v for k, v in _L0_conv_all.items() if k in ('w_theta', 'w_phi', 'w_g', 'w_o', 'b_o', 'sigma')}
    del _L0_conv_all

    def _L1_conv_setup():
        import jax, jax.numpy as jnp
        import numpy as np
        EPS = 1e-05
        D_CONV = 4

        def rmsnorm(x, w):
            return x * jax.lax.rsqrt(jnp.mean(x * x, axis=-1, keepdims=True) + EPS) * w

        def layernorm(x, w, b):
            m = jnp.mean(x, axis=-1, keepdims=True)
            v = jnp.mean((x - m) ** 2, axis=-1, keepdims=True)
            return (x - m) * jax.lax.rsqrt(v + EPS) * w + b

        def mamba_mixer(x, W_in, conv_w, conv_b, W_x, W_dt, b_dt, A_log, Dp, W_out):
            B, L, C = x.shape
            I = W_out.shape[1]
            N = A_log.shape[1]
            R = W_dt.shape[1]
            proj = x @ W_in.T
            hs, gate = jnp.split(proj, 2, axis=-1)
            hs_c = jax.lax.conv_general_dilated(hs.transpose(0, 2, 1), conv_w, (1,), [(D_CONV - 1, 0)], dimension_numbers=('NCH', 'OIH', 'NCH'), feature_group_count=I)
            hs = jax.nn.silu(hs_c.transpose(0, 2, 1) + conv_b)
            ssm_in = hs @ W_x.T
            dt_r, Bm, Cm = jnp.split(ssm_in, [R, R + N], axis=-1)
            dt = jax.nn.softplus(dt_r @ W_dt.T + b_dt)
            A = -jnp.exp(A_log)

            def step(state, inp):
                dt_t, B_t, C_t, u_t = inp
                dA = jnp.exp(dt_t[:, :, None] * A)
                state = dA * state + dt_t[:, :, None] * B_t[:, None, :] * u_t[:, :, None]
                y = jnp.einsum('bin,bn->bi', state, C_t)
                return (state, y)
            xs = (dt.transpose(1, 0, 2), Bm.transpose(1, 0, 2), Cm.transpose(1, 0, 2), hs.transpose(1, 0, 2))
            state0 = jnp.zeros((B, I, N), x.dtype)
            _, ys = jax.lax.scan(step, state0, xs)
            y = ys.transpose(1, 0, 2) + hs * Dp
            y = y * jax.nn.silu(gate)
            return y @ W_out.T

        def forward_scan(x, W_in, conv_w, conv_b, W_x, W_dt, b_dt, A_log, Dp, W_out, rms_w1, rms_wf):
            h = x + mamba_mixer(rmsnorm(x, rms_w1), W_in, conv_w, conv_b, W_x, W_dt, b_dt, A_log, Dp, W_out)
            return rmsnorm(h, rms_wf)
        key = jax.random.key(seed)
        ks = jax.random.split(key, 12)
        BT, H, W, C = (8, 32, 32, 64)
        I, N, R = (2 * C, 16, 16)
        s = 0.02
        x = jax.random.normal(ks[0], (BT, H, W, C), jnp.float32)
        W_in = jax.random.normal(ks[1], (2 * I, C), jnp.float32) * s
        conv_w = jax.random.normal(ks[2], (I, 1, D_CONV), jnp.float32) * s
        conv_b = jax.random.normal(ks[3], (I,), jnp.float32) * s
        W_x = jax.random.normal(ks[4], (R + 2 * N, I), jnp.float32) * s
        W_dt = jax.random.normal(ks[5], (I, R), jnp.float32) * s
        b_dt = jax.random.normal(ks[6], (I,), jnp.float32) * 0.1
        A_log = jnp.log(jnp.broadcast_to(jnp.arange(1, N + 1, dtype=jnp.float32), (I, N)))
        Dp = jnp.ones((I,), jnp.float32)
        W_out = jax.random.normal(ks[7], (C, I), jnp.float32) * s
        rms_w1 = jnp.ones((C,), jnp.float32)
        rms_wf = jnp.ones((C,), jnp.float32)
        ln_w = jnp.ones((C,), jnp.float32)
        ln_b = jnp.zeros((C,), jnp.float32)
        return {'x': x, 'W_in': W_in, 'conv_w': conv_w, 'conv_b': conv_b, 'W_x': W_x, 'W_dt': W_dt, 'b_dt': b_dt, 'A_log': A_log, 'Dp': Dp, 'W_out': W_out, 'rms_w1': rms_w1, 'rms_wf': rms_wf, 'ln_w': ln_w, 'ln_b': ln_b}
    _L1_conv_all = _L1_conv_setup()
    _L1_conv_in = {k: v for k, v in _L1_conv_all.items() if k in ('W_in', 'conv_w', 'conv_b', 'W_x', 'W_dt', 'b_dt', 'A_log', 'Dp', 'W_out', 'rms_w1', 'rms_wf', 'ln_w', 'ln_b')}
    del _L1_conv_all
    return {'x': x, 'L0_conv_w_theta': _L0_conv_in['w_theta'], 'L0_conv_w_phi': _L0_conv_in['w_phi'], 'L0_conv_w_g': _L0_conv_in['w_g'], 'L0_conv_w_o': _L0_conv_in['w_o'], 'L0_conv_b_o': _L0_conv_in['b_o'], 'L0_conv_sigma': _L0_conv_in['sigma'], 'L1_conv_W_in': _L1_conv_in['W_in'], 'L1_conv_conv_w': _L1_conv_in['conv_w'], 'L1_conv_conv_b': _L1_conv_in['conv_b'], 'L1_conv_W_x': _L1_conv_in['W_x'], 'L1_conv_W_dt': _L1_conv_in['W_dt'], 'L1_conv_b_dt': _L1_conv_in['b_dt'], 'L1_conv_A_log': _L1_conv_in['A_log'], 'L1_conv_Dp': _L1_conv_in['Dp'], 'L1_conv_W_out': _L1_conv_in['W_out'], 'L1_conv_rms_w1': _L1_conv_in['rms_w1'], 'L1_conv_rms_wf': _L1_conv_in['rms_wf'], 'L1_conv_ln_w': _L1_conv_in['ln_w'], 'L1_conv_ln_b': _L1_conv_in['ln_b']}

def reference(x, L0_conv_w_theta, L0_conv_w_phi, L0_conv_w_g, L0_conv_w_o, L0_conv_b_o, L0_conv_sigma, L1_conv_W_in, L1_conv_conv_w, L1_conv_conv_b, L1_conv_W_x, L1_conv_W_dt, L1_conv_b_dt, L1_conv_A_log, L1_conv_Dp, L1_conv_W_out, L1_conv_rms_w1, L1_conv_rms_wf, L1_conv_ln_w, L1_conv_ln_b):
    import jax
    import jax.numpy as jnp

    def _L0_conv_ref(x, w_theta, w_phi, w_g, w_o, b_o, sigma):
        import jax, jax.numpy as jnp
        import numpy as np

        def _maxpool2x2(t):
            B, H, W, C = t.shape
            return t.reshape(B, H // 2, 2, W // 2, 2, C).max(axis=(2, 4))
        B, H, W, C = x.shape
        L = H * W
        Ld = L // 4
        theta = jnp.einsum('bhwc,cd->bhwd', x, w_theta).reshape(B, L, C // 8)
        phi = jnp.einsum('bhwc,cd->bhwd', x, w_phi)
        phi = _maxpool2x2(phi).reshape(B, Ld, C // 8)
        attn = jax.nn.softmax(jnp.einsum('bld,bmd->blm', theta, phi), axis=-1)
        g = jnp.einsum('bhwc,cd->bhwd', x, w_g)
        g = _maxpool2x2(g).reshape(B, Ld, C // 2)
        attn_g = jnp.einsum('blm,bmd->bld', attn, g).reshape(B, H, W, C // 2)
        attn_g = jnp.einsum('bhwd,dc->bhwc', attn_g, w_o) + b_o
        return x + sigma * attn_g

    def _L1_conv_ref(x, W_in, conv_w, conv_b, W_x, W_dt, b_dt, A_log, Dp, W_out, rms_w1, rms_wf, ln_w, ln_b):
        import jax, jax.numpy as jnp
        import numpy as np
        EPS = 1e-05
        D_CONV = 4

        def rmsnorm(x, w):
            return x * jax.lax.rsqrt(jnp.mean(x * x, axis=-1, keepdims=True) + EPS) * w

        def layernorm(x, w, b):
            m = jnp.mean(x, axis=-1, keepdims=True)
            v = jnp.mean((x - m) ** 2, axis=-1, keepdims=True)
            return (x - m) * jax.lax.rsqrt(v + EPS) * w + b

        def mamba_mixer(x, W_in, conv_w, conv_b, W_x, W_dt, b_dt, A_log, Dp, W_out):
            B, L, C = x.shape
            I = W_out.shape[1]
            N = A_log.shape[1]
            R = W_dt.shape[1]
            proj = x @ W_in.T
            hs, gate = jnp.split(proj, 2, axis=-1)
            hs_c = jax.lax.conv_general_dilated(hs.transpose(0, 2, 1), conv_w, (1,), [(D_CONV - 1, 0)], dimension_numbers=('NCH', 'OIH', 'NCH'), feature_group_count=I)
            hs = jax.nn.silu(hs_c.transpose(0, 2, 1) + conv_b)
            ssm_in = hs @ W_x.T
            dt_r, Bm, Cm = jnp.split(ssm_in, [R, R + N], axis=-1)
            dt = jax.nn.softplus(dt_r @ W_dt.T + b_dt)
            A = -jnp.exp(A_log)

            def step(state, inp):
                dt_t, B_t, C_t, u_t = inp
                dA = jnp.exp(dt_t[:, :, None] * A)
                state = dA * state + dt_t[:, :, None] * B_t[:, None, :] * u_t[:, :, None]
                y = jnp.einsum('bin,bn->bi', state, C_t)
                return (state, y)
            xs = (dt.transpose(1, 0, 2), Bm.transpose(1, 0, 2), Cm.transpose(1, 0, 2), hs.transpose(1, 0, 2))
            state0 = jnp.zeros((B, I, N), x.dtype)
            _, ys = jax.lax.scan(step, state0, xs)
            y = ys.transpose(1, 0, 2) + hs * Dp
            y = y * jax.nn.silu(gate)
            return y @ W_out.T

        def forward_scan(x, W_in, conv_w, conv_b, W_x, W_dt, b_dt, A_log, Dp, W_out, rms_w1, rms_wf):
            h = x + mamba_mixer(rmsnorm(x, rms_w1), W_in, conv_w, conv_b, W_x, W_dt, b_dt, A_log, Dp, W_out)
            return rmsnorm(h, rms_wf)
        BT, H, W, C = x.shape
        xs = jnp.stack([x, x[:, :, ::-1], x[:, ::-1], x[:, ::-1, ::-1]], axis=0)
        xs = xs.reshape(4 * BT, H * W, C)
        out = forward_scan(xs, W_in, conv_w, conv_b, W_x, W_dt, b_dt, A_log, Dp, W_out, rms_w1, rms_wf)
        out = out.reshape(4, BT, H, W, C)
        o = (out[0] + out[1][:, :, ::-1] + out[2][:, ::-1] + out[3][:, ::-1, ::-1]) / 4.0
        return layernorm(o, ln_w, ln_b)

    def _gn(v, G=32, eps=1e-05):
        B_, H_, W_, C_ = v.shape
        g = v.reshape(B_, H_, W_, G, C_ // G)
        m = jnp.mean(g, axis=(1, 2, 4), keepdims=True)
        s = jnp.var(g, axis=(1, 2, 4), keepdims=True)
        return ((g - m) / jnp.sqrt(s + eps)).reshape(v.shape)

    def _ln_c(v, eps=1e-06):
        m = jnp.mean(v, axis=-1, keepdims=True)
        s = jnp.var(v, axis=-1, keepdims=True)
        return (v - m) / jnp.sqrt(s + eps)

    def _ln_t(v, eps=1e-05):
        m = jnp.mean(v, axis=-1, keepdims=True)
        s = jnp.var(v, axis=-1, keepdims=True)
        return (v - m) / jnp.sqrt(s + eps)

    def _to_tokens(v):
        B_, H_, W_, C_ = v.shape
        return v.reshape(B_, H_ * W_, C_)

    def _from_tokens(t, like):
        return t.reshape(like.shape)
    x = _L0_conv_ref(x, L0_conv_w_theta, L0_conv_w_phi, L0_conv_w_g, L0_conv_w_o, L0_conv_b_o, L0_conv_sigma)
    x = _L1_conv_ref(x, L1_conv_W_in, L1_conv_conv_w, L1_conv_conv_b, L1_conv_W_x, L1_conv_W_dt, L1_conv_b_dt, L1_conv_A_log, L1_conv_Dp, L1_conv_W_out, L1_conv_rms_w1, L1_conv_rms_wf, L1_conv_ln_w, L1_conv_ln_b)
    return x

_drawn_inputs = setup_inputs


def setup_inputs(seed=0):
    import zlib

    import numpy as np

    out = dict(_drawn_inputs(seed))
    spreads = {'L0_conv_b_o': (0.0, 0.1),
     'L1_conv_Dp': (1.0, 0.6),
     'L1_conv_rms_w1': (1.0, 0.6),
     'L1_conv_rms_wf': (1.0, 0.2),
     'L1_conv_ln_w': (1.0, 0.2),
     'L1_conv_ln_b': (0.0, 0.1)}
    factors = {'L0_conv_w_theta': 8.0,
     'L0_conv_w_phi': 8.0,
     'L0_conv_w_g': 6.569,
     'L1_conv_W_in': 8.0,
     'L1_conv_conv_w': 8.0,
     'L1_conv_conv_b': 8.0,
     'L1_conv_W_x': 8.0,
     'L1_conv_W_dt': 8.0,
     'L1_conv_b_dt': 8.0,
     'L1_conv_A_log': 8.0,
     'L1_conv_W_out': 8.0}
    for name, (base, spread) in spreads.items():
        noise = np.random.default_rng([zlib.crc32(name.encode()), seed]).standard_normal(out[name].shape)
        drawn = base * np.exp(spread * noise) if base else spread * noise
        out[name] = jnp.asarray(drawn.astype(out[name].dtype))
    for name, factor in factors.items():
        out[name] = (out[name] * factor).astype(out[name].dtype)
    return out
```

```python
import concourse.bass as bass
from concourse import mybir
from contextlib import ExitStack

F32 = mybir.dt.float32
BF16 = mybir.dt.bfloat16
ALU = mybir.AluOpType
ACT = mybir.ActivationFunctionType
AX = mybir.AxisListType

IMAGES, SIDE, C = 16, 16, 64
L = SIDE * SIDE
POOLED = L // 4
KEY, VAL = C // 8, C // 2
I = 2 * C
N = 16
R = 16
TAPS = 4
DIRS = 4
T = DIRS * L
HALF = T // 2
CHUNKS = L // 128
PADDED = L + 4
EPS = 1e-5
COPIES = 3
SPLIT_ROWS = 32 * COPIES
C_ROW = SPLIT_ROWS
A_RING, H_RING, C_RING = 4, 8, 4


class Image:

    def __init__(self, pair, offset):
        self.pair, self.offset = pair, offset
        self.num = 2 * pair + offset
        self.buf = offset % 2

    def __add__(self, d):
        return Image(self.pair, self.offset + d)


def at_least(eng, sem, value):
    if not isinstance(value, int) or value > 0:
        eng.wait_ge(sem, value)


def all_at_least(eng, *waits):
    values = [v if isinstance(v, int) else eng.snap(eng.to_reg(v)) for _, v in waits]
    for (sem, _), value in zip(waits, values):
        at_least(eng, sem, value)


def build(nc, a, out):
    ctx = ExitStack()
    with ctx:
        def sb(name, shape, dt=F32):
            return ctx.enter_context(nc.sbuf_tensor(name, shape, dt))

        def ps(name, shape):
            return ctx.enter_context(nc.psum_tensor(name, shape, F32))

        def sem(name):
            return ctx.enter_context(nc.semaphore(name))

        ident = sb("ident", [128, 128])
        w_qkv = sb("w_qkv", [2 * C, 2 * KEY + VAL])
        w_o2 = sb("w_o2", [VAL, 2 * C])
        sigma = sb("sigma", [128, 1])
        b_o2 = sb("b_o2", [128, 1])
        sigma_b = sb("sigma_b", [128, 1])
        w_in2 = sb("w_in2", [128, 2 * I])
        rms1 = sb("rms1", [128, 1])
        tap_rows = sb("tap_rows", [128, 2, I])
        w_conv = sb("w_conv", [128, 2, I])
        w_gate = sb("w_gate", [2 * C, I])
        conv_b = sb("conv_b", [I, 1])
        b_dt = sb("b_dt", [I, 1])
        d_skip = sb("d_skip", [I, 1])
        diag_d = sb("diag_d", [I, I])
        a_log = sb("a_log", [I, N])
        a_exp = sb("a_exp", [I, N])
        a_neg = sb("a_neg", [I, N])
        w_bc = sb("w_bc", [I, C_ROW + N])
        w_x_dt = sb("w_x_dt", [R, I])
        w_dt = sb("w_dt", [R, I])
        w_step = sb("w_step", [I, I])
        w_out = sb("w_out", [I, C])
        wf_rows = sb("wf_rows", [128, C])
        wf4_rows = sb("wf4_rows", [128, C])
        ln_w_rows = sb("ln_w_rows", [128, C])
        ln_b_rows = sb("ln_b_rows", [128, C])
        mean_w = sb("mean_w", [C, 128])
        eps = sb("eps", [128, 1])
        one = sb("one", [128, 1])
        onehot = sb("onehot", [SPLIT_ROWS, N])
        pick_b = sb("pick_b", [SPLIT_ROWS, N, 128], BF16)

        xt = sb("xt", [128, L])
        xb = sb("xb", [128, L])
        theta = sb("theta", [KEY, L])
        phi_p = sb("phi_p", [KEY, POOLED])
        g_p = sb("g_p", [VAL, POOLED])
        gw = sb("gw", [POOLED, 2 * C])
        nmax = sb("nmax", [128, CHUNKS])
        esc = sb("esc", [128, CHUNKS, POOLED])
        esum = sb("esum", [128, CHUNKS])
        erec = sb("erec", [128, CHUNKS])
        attn = sb("attn", [128, CHUNKS, POOLED])
        attn_t = sb("attn_t", [POOLED, L])
        x2 = [sb(f"x2_{q}", [128, L]) for q in range(2)]
        x2sq = sb("x2sq", [C, L])
        ln1 = sb("ln1", [128, L])
        rinv1 = sb("rinv1", [128, L])
        xn = [sb(f"xn_{q}", [128, L]) for q in range(2)]
        xpad = sb("xpad", [128, DIRS, PADDED])
        u = [sb(f"u_{q}", [I, T]) for q in range(2)]
        gate = [sb(f"gate_{q}", [I, L]) for q in range(2)]
        x2l = [sb(f"x2l_{q}", [128, CHUNKS * C]) for q in range(2)]
        absx = sb("absx", [I, T])
        relx = sb("relx", [I, T])
        expx = sb("expx", [I, T])
        lnx = sb("lnx", [I, T])
        rounded = sb("rounded", [I, T])
        step = [sb(f"step_{q}", [I, T]) for q in range(2)]
        du = [sb(f"du_{q}", [I, T]) for q in range(2)]
        b_parts = [sb(f"b_parts_{q}", [SPLIT_ROWS, T], BF16) for q in range(2)]
        b_rest = sb("b_rest", [64, T])
        c_rows = sb("c_rows", [128, T])
        decay = [sb(f"decay_{r}", [I, DIRS, L]) for r in range(A_RING)]
        state = [sb(f"state_{r}", [I, T]) for r in range(H_RING)]
        c_all = [sb(f"c_all_{r}", [I, T]) for r in range(C_RING)]
        yg = sb("yg", [I, DIRS, L])
        hid = sb("hid", [128, DIRS, CHUNKS * C])
        hidsq = sb("hidsq", [128, DIRS * CHUNKS, C])
        hsum = sb("hsum", [128, DIRS * CHUNKS])
        hln = sb("hln", [128, DIRS * CHUNKS])
        hinv = sb("hinv", [128, DIRS * CHUNKS])
        hnorm = sb("hnorm", [128, DIRS * CHUNKS, C])
        osum = sb("osum", [128, CHUNKS, C])
        oavg = sb("oavg", [128, CHUNKS, C])
        omean = sb("omean", [128, CHUNKS])
        ocen = sb("ocen", [128, CHUNKS, C])
        osq = sb("osq", [128, CHUNKS, C])
        ovar = sb("ovar", [128, CHUNKS])
        oln = sb("oln", [128, CHUNKS])
        oinv = sb("oinv", [128, CHUNKS])
        onorm = sb("onorm", [128, CHUNKS, C])
        oscaled = sb("oscaled", [128, CHUNKS, C])
        ofin = sb("ofin", [128, CHUNKS, C])

        ps_b = [ps(f"ps_b{q}", [128, T]) for q in range(2)]
        ps_y = ps("ps_y", [128, T])
        ps_w = ps("ps_w", [128, T])
        w0, w1 = ps_w[:, 0:HALF], ps_w[:, HALF:T]

        c_dram = [nc.dram_tensor(f"c_dram_{q}", [N, T], F32, kind="Internal").ap() for q in range(2)]

        weights_in = sem("weights_in")
        zeroed = sem("zeroed")
        wbc_zeroed = sem("wbc_zeroed")
        a_exp_done = sem("a_exp_done")
        step_w_done = sem("step_w_done")
        weights_ready = sem("weights_ready")
        x_loaded = sem("x_loaded")
        xb_done = sem("xb_done")
        qkv_done = sem("qkv_done")
        pooled_done = sem("pooled_done")
        scores_done = sem("scores_done")
        nmax_done = sem("nmax_done")
        gw_done = sem("gw_done")
        esc_done = sem("esc_done")
        erec_done = sem("erec_done")
        attn_done = sem("attn_done")
        attn_t_ps = sem("attn_t_ps")
        attn_t_done = sem("attn_t_done")
        o_done = sem("o_done")
        x2_done = sem("x2_done")
        x2sq_done = sem("x2sq_done")
        ms_done = sem("ms_done")
        ln1_done = sem("ln1_done")
        rinv1_done = sem("rinv1_done")
        xn_done = sem("xn_done")
        padded = sem("padded")
        conv_done = sem("conv_done")
        u_done = sem("u_done")
        gate_mm = sem("gate_mm")
        gate_done = sem("gate_done")
        step_mm = sem("step_mm")
        absx_done = sem("absx_done")
        relx_done = sem("relx_done")
        expx_done = sem("expx_done")
        lnx_done = sem("lnx_done")
        rounded_done = sem("rounded_done")
        rest_done = sem("rest_done")
        soft_done = sem("soft_done")
        step_done = sem("step_done")
        du_done = sem("du_done")
        bc_mm = sem("bc_mm")
        hi_done = sem("hi_done")
        c_rows_done = sem("c_rows_done")
        b_rest_done = sem("b_rest_done")
        mid_done = sem("mid_done")
        lo_done = sem("lo_done")
        c_stored = sem("c_stored")
        x2l_ps = sem("x2l_ps")
        x2l_done = sem("x2l_done")
        decay_done = sem("decay_done")
        b_all_done = sem("b_all_done")
        input_done = sem("input_done")
        scans = sem("scans")
        c_loaded = [sem(f"c_loaded{r}") for r in range(C_RING)]
        products = sem("products")
        sums = sem("sums")
        yg_done = sem("yg_done")
        out_mm = sem("out_mm")
        hid_done = sem("hid_done")
        hidsq_done = sem("hidsq_done")
        hsum_done = sem("hsum_done")
        hln_done = sem("hln_done")
        hinv_done = sem("hinv_done")
        hnorm_done = sem("hnorm_done")
        osum_done = sem("osum_done")
        oavg_done = sem("oavg_done")
        omean_done = sem("omean_done")
        ocen_done = sem("ocen_done")
        osq_done = sem("osq_done")
        ovar_done = sem("ovar_done")
        oln_done = sem("oln_done")
        oinv_done = sem("oinv_done")
        onorm_done = sem("onorm_done")
        oscaled_done = sem("oscaled_done")
        ofin_done = sem("ofin_done")
        stored = sem("stored")

        def ordered(view, d):
            v = view.rearrange("p (h w) -> p h w", h=SIDE)
            if d in (2, 3):
                v = v[:, ::-1, :]
            if d in (1, 3):
                v = v[:, :, ::-1]
            return v

        def grid(view):
            return view.rearrange("p (h w) -> p h w", h=SIDE)

        column = lambda v: v.rearrange("(p a) -> p a", a=1)
        loads = [
            (ident[:, :], a["ident"]),
            (w_qkv[0:C, 0:KEY], a["w_theta"]),
            (w_qkv[0:C, KEY:2 * KEY], a["w_phi"]),
            (w_qkv[0:C, 2 * KEY:], a["w_g"]),
            (w_o2[:, 0:C], a["w_o"]),
            (w_o2[:, C:], a["w_o"]),
            (sigma[:, :], a["sigma"].partition_broadcast(128)),
            (b_o2[0:C, :], column(a["b_o"])),
            (b_o2[C:, :], column(a["b_o"])),
            (w_in2[0:C, :], a["w_in_t"]),
            (w_in2[C:, :], a["w_in_t"]),
            (rms1[0:C, :], column(a["rms_w1"])),
            (rms1[C:, :], column(a["rms_w1"])),
            (tap_rows[0:C, 0, :], a["conv_w_t"][0, :].partition_broadcast(C)),
            (tap_rows[C:, 0, :], a["conv_w_t"][1, :].partition_broadcast(C)),
            (tap_rows[0:C, 1, :], a["conv_w_t"][2, :].partition_broadcast(C)),
            (tap_rows[C:, 1, :], a["conv_w_t"][3, :].partition_broadcast(C)),
            (conv_b[:, :], column(a["conv_b"])),
            (b_dt[:, :], column(a["b_dt"])),
            (d_skip[:, :], column(a["Dp"])),
            (a_log[:, :], a["A_log"]),
            (w_x_dt[:, :], a["W_x"][0:R, :]),
            (w_dt[:, :], a["w_dt_t"]),
            (w_out[:, :], a["w_out_t"]),
            (wf_rows[:, :], a["rms_wf"].partition_broadcast(128)),
            (ln_w_rows[:, :], a["ln_w"].partition_broadcast(128)),
            (ln_b_rows[:, :], a["ln_b"].partition_broadcast(128)),
            (onehot[:, :], a["onehot"]),
        ]
        w_bc_loads = [(w_bc[:, 32 * k:32 * k + N], a["w_x_t"][:, R:R + N]) for k in range(COPIES)]
        w_bc_loads.append((w_bc[:, C_ROW:C_ROW + N], a["w_x_t"][:, R + N:]))
        N_LOADS = len(loads) + len(w_bc_loads)

        block = ctx.enter_context(nc.Block())

        def program(eng, setup, attend, project, steps, finish):
            setup()
            first = Image(0, 0)
            for part in attend(first):
                part()
            for part in project(first):
                part()
            for part in attend(first + 1):
                part()
            steps(first, None, first + 1, first + 2)
            steps(first + 1, first, first + 2, first + 3)
            with eng.Fori(0, (IMAGES - 4) // 2) as pair:
                for offset in (2, 3):
                    b = Image(pair, offset)
                    steps(b, b + -1, b + 1, b + 2)
            last = Image(0, IMAGES - 1)
            steps(last + -1, last + -2, last, None)
            steps(last, last + -1, None, None)
            for part in finish(last):
                part()

        @block.sync
        def _(sp):
            def setup():
                for dst, src in loads:
                    sp.dma_start(dst, src).then_inc(weights_in, 16)
                sp.wait_ge(wbc_zeroed, 1)
                for dst, src in w_bc_loads:
                    sp.dma_start(dst, src).then_inc(weights_in, 16)

            def load_x(j):
                all_at_least(sp, (xb_done, j.num), (qkv_done, j.num))
                sp.wait_ge(weights_ready, 1)
                for half in range(2):
                    sp.dma_start(xt[C * half:C * half + C, :], a["x_t"][j.num, :, :]).then_inc(x_loaded, 16)

            def store_c(j):
                all_at_least(sp, (c_rows_done, j.num + 1), (products, N * (j.num - 1)))
                sp.dma_start(c_dram[j.buf], c_rows[C_ROW:C_ROW + N, :]).then_inc(c_stored, 16)

            def load_c(b, n):
                stored_c = [(c_stored, 16 * (b.num + 1))] if n == 0 else []
                all_at_least(sp, *stored_c, (products, N * b.num + n - C_RING + 1))
                sp.dma_start(c_all[n % C_RING][:, :], c_dram[b.buf][n, :].partition_broadcast(128)
                             ).then_inc(c_loaded[n % C_RING], 16)

            def store_out(j):
                sp.wait_ge(ofin_done, j.num + 1)
                sp.wait_ge(weights_ready, 1)
                sp.dma_start(out[j.num, :, :].rearrange("(k p) c -> p k c", p=128), ofin[:, :, :]
                             ).then_inc(stored, 16)

            def attend(j):
                return [lambda: load_x(j)]

            def project(j):
                return [lambda: store_c(j)]

            def finish(j):
                return [lambda: store_out(j)]

            def steps(b, done, coming, later):
                for n in range(N):
                    load_c(b, n)
                    if n == 3 and later:
                        load_x(later)
                    if n == 11 and coming:
                        store_c(coming)
                    if n == 15 and done:
                        store_out(done)

            program(sp, setup, attend, project, steps, finish)
            sp.wait_ge(stored, 16 * IMAGES)

        @block.tensor
        def _(pe):
            mm = nc.tensor.matmul

            def setup():
                pe.wait_ge(weights_in, 16 * N_LOADS)
                mm(w0[:, 0:I], w_x_dt[:, :], w_dt[:, :], start=True, stop=True).then_inc(step_w_done, 1)
                pe.wait_ge(weights_ready, 1)

            def qkv(j):
                pe.wait_ge(x_loaded, 32 * (j.num + 1))
                at_least(pe, x2l_done, j.num)
                mm(w0[0:KEY, 0:L], w_qkv[:, 0:KEY], xt[:, :], start=True, stop=True)
                mm(w0[0:KEY, L:2 * L], w_qkv[:, KEY:2 * KEY], xt[:, :], start=True, stop=True)
                mm(w1[0:VAL, 0:L], w_qkv[:, 2 * KEY:], xt[:, :], start=True, stop=True
                   ).then_inc(qkv_done, 1)

            def scores(j):
                pe.wait_ge(pooled_done, j.num + 1)
                for k in range(CHUNKS):
                    mm(w0[:, POOLED * k:POOLED * (k + 1)], theta[:, 128 * k:128 * (k + 1)], phi_p[:, :],
                       start=True, stop=True)
                mm(w1[0:POOLED, 0:2 * C], g_p[:, :], w_o2[:, :], start=True, stop=True
                   ).then_inc(scores_done, 1)

            def attn_turn(j):
                pe.wait_ge(attn_done, j.num + 1)
                for k in range(CHUNKS):
                    last = mm(w0[0:POOLED, 128 * k:128 * (k + 1)], attn[:, k, :], ident[:, :], start=True, stop=True)
                last.then_inc(attn_t_ps, 1)

            def attn_out(j):
                pe.wait_ge(attn_t_done, j.num + 1)
                pe.wait_ge(gw_done, j.num + 1)
                mm(w1[:, 0:L], gw[:, :], attn_t[:, :], start=True, stop=True).then_inc(o_done, 1)

            def mean_square(j):
                pe.wait_ge(x2sq_done, j.num + 1)
                mm(w0[:, 0:L], mean_w[:, :], x2sq[:, :], start=True, stop=True).then_inc(ms_done, 1)

            def conv(j):
                pe.wait_ge(padded, 2 * DIRS * (j.num + 1))
                at_least(pe, hid_done, j.num - 2)
                for half in range(2):
                    for tap2 in range(2):
                        last = mm(ps_w[:, HALF * half:HALF * (half + 1)], w_conv[:, tap2, :],
                                  xpad[:, 2 * half:2 * half + 2, 2 * tap2:2 * tap2 + L],
                                  start=(tap2 == 0), stop=(tap2 == 1))
                last.then_inc(conv_done, 1)

            def gate_proj(j):
                pe.wait_ge(u_done, j.num + 1)
                mm(w0[:, 0:L], w_gate[:, :], xn[j.buf][:, :], start=True, stop=True).then_inc(gate_mm, 1)

            def step_proj(j):
                pe.wait_ge(gate_done, j.num + 1)
                at_least(pe, hid_done, j.num - 1)
                for half in range(2):
                    last = mm(ps_w[:, HALF * half:HALF * (half + 1)], w_step[:, :],
                              u[j.buf][:, HALF * half:HALF * (half + 1)], start=True, stop=True)
                last.then_inc(step_mm, 1)

            def bc_proj(j):
                pe.wait_ge(relx_done, j.num + 1)
                for half in range(2):
                    last = mm(ps_w[0:C_ROW + N, HALF * half:HALF * (half + 1)], w_bc[:, :],
                              u[j.buf][:, HALF * half:HALF * (half + 1)], start=True, stop=True)
                last.then_inc(bc_mm, 1)

            def x2_turn(j):
                pe.wait_ge(b_rest_done, j.num + 1)
                pe.wait_ge(c_rows_done, j.num + 1)
                for k in range(CHUNKS):
                    last = mm(w0[:, C * k:C * (k + 1)], x2[j.buf][0:C, 128 * k:128 * (k + 1)], ident[0:C, 0:C],
                              start=True, stop=True)
                last.then_inc(x2l_ps, 1)

            def out_proj(j):
                pe.wait_ge(yg_done, DIRS * (j.num + 1))
                at_least(pe, u_done, j.num + 3 if j.offset < IMAGES - 2 else 0)
                if j.offset >= IMAGES - 2:
                    pe.wait_ge(x2l_done, IMAGES)
                    at_least(pe, hid_done, j.num if j.offset == IMAGES - 1 else 0)
                for d in range(DIRS):
                    for k in range(CHUNKS):
                        m = CHUNKS * d + k
                        last = mm(w1[:, C * m:C * (m + 1)], yg[:, d, 128 * k:128 * (k + 1)], w_out[:, :],
                                  start=True, stop=True)
                last.then_inc(out_mm, 1)

            def spread_b(b, n):
                if n == 0:
                    pe.wait_ge(lo_done, b.num + 1)
                at_least(pe, scans, N * b.num + n - 1)
                for half in range(2):
                    last = mm(ps_b[n % 2][:, HALF * half:HALF * (half + 1)], pick_b[:, n, :],
                              b_parts[b.buf][:, HALF * half:HALF * (half + 1)], start=True, stop=True)
                last.then_inc(b_all_done, 1)

            def skip(b):
                at_least(pe, yg_done, DIRS * b.num)
                for half in range(2):
                    mm(ps_y[:, HALF * half:HALF * (half + 1)], diag_d[:, :],
                       u[b.buf][:, HALF * half:HALF * (half + 1)], start=True, stop=False)

            def sum_state(b, n):
                pe.wait_ge(products, N * b.num + n + 1)
                for half in range(2):
                    last = mm(ps_y[:, HALF * half:HALF * (half + 1)], ident[:, :],
                              state[n % H_RING][:, HALF * half:HALF * (half + 1)],
                              start=False, stop=(n == N - 1))
                last.then_inc(sums, 1)

            def attend(j):
                return [lambda f=f: f(j) for f in (qkv, scores, attn_turn, attn_out, mean_square)]

            def project(j):
                return [lambda f=f: f(j) for f in (conv, gate_proj, step_proj, bc_proj, x2_turn)]

            def finish(j):
                return [lambda: sum_state(j, N - 2), lambda: sum_state(j, N - 1), lambda: out_proj(j)]

            def steps(b, done, coming, later):
                for n in range(N):
                    spread_b(b, n)
                    if n == 0 and done:
                        sum_state(done, N - 2)
                    if n == 1 and done:
                        sum_state(done, N - 1)
                    if n == 1 and coming:
                        conv(coming)
                    if n == 2 and coming:
                        gate_proj(coming)
                    if n == 3:
                        skip(b)
                        sum_state(b, 0)
                    if n == 3 and done:
                        out_proj(done)
                    if n == 4:
                        sum_state(b, 1)
                    if n >= 4:
                        sum_state(b, n - 2)
                    if n == 4 and coming:
                        step_proj(coming)
                    if n == 5 and coming:
                        bc_proj(coming)
                    if n == 7 and coming:
                        x2_turn(coming)
                    if n == 9 and later:
                        qkv(later)
                    if n == 10 and later:
                        scores(later)
                    if n == 12 and later:
                        attn_turn(later)
                    if n == 13 and later:
                        attn_out(later)
                    if n == 14 and later:
                        mean_square(later)

            program(pe, setup, attend, project, steps, finish)

        @block.scalar
        def _(act):
            f = nc.scalar.activation

            def setup():
                act.wait_ge(weights_in, 16 * N_LOADS)
                f(a_exp[:, :], a_log[:, :], ACT.Exp).then_inc(a_exp_done, 1)
                act.wait_ge(weights_ready, 1)

            def add_bias(j):
                act.wait_ge(x_loaded, 32 * (j.num + 1))
                at_least(act, x2_done, j.num)
                f(xb[:, :], xt[:, :], ACT.Identity, bias=sigma_b[:, :]).then_inc(xb_done, 1)

            def softmax_exp(j):
                act.wait_ge(nmax_done, j.num + 1)
                at_least(act, attn_done, j.num)
                for k in range(CHUNKS):
                    last = f(esc[:, k, :], w0[:, POOLED * k:POOLED * (k + 1)], ACT.Exp, bias=nmax[:, k:k + 1],
                             accum_out=esum[:, k:k + 1])
                last.then_inc(esc_done, 1)

            def attn_copy(j):
                act.wait_ge(attn_t_ps, j.num + 1)
                at_least(act, o_done, j.num)
                f(attn_t[:, :], w0[0:POOLED, 0:L], ACT.Copy).then_inc(attn_t_done, 1)

            def square(j):
                act.wait_ge(x2_done, j.num + 1)
                at_least(act, ms_done, j.num)
                f(x2sq[:, :], x2[j.buf][0:C, :], ACT.Square).then_inc(x2sq_done, 1)

            def rms_inverse(j):
                act.wait_ge(ms_done, j.num + 1)
                f(ln1[:, :], w0[:, 0:L], ACT.Ln, bias=eps[:, :]).then_inc(ln1_done, 1)
                at_least(act, xn_done, j.num)
                act.wait_ge(ln1_done, j.num + 1)
                f(rinv1[:, :], ln1[:, :], ACT.Exp, scale=-0.5).then_inc(rinv1_done, 1)

            def pad(j):
                act.wait_ge(xn_done, j.num + 1)
                at_least(act, conv_done, j.num)
                for d in range(DIRS):
                    f(grid(xpad[0:C, d, 3:3 + L]), ordered(xn[j.buf][0:C, :], d), ACT.Copy).then_inc(padded, 1)
                    f(grid(xpad[C:, d, 2:2 + L]), ordered(xn[j.buf][C:, :], d), ACT.Copy).then_inc(padded, 1)

            def conv_silu(j):
                act.wait_ge(conv_done, j.num + 1)
                at_least(act, sums, N * (j.num - 1))
                at_least(act, du_done, j.num - 1)
                f(u[j.buf][:, :], ps_w[:, :], ACT.Silu, bias=conv_b[:, :]).then_inc(u_done, 1)

            def gate_silu(j):
                act.wait_ge(gate_mm, j.num + 1)
                at_least(act, yg_done, DIRS * (j.num - 1))
                f(gate[j.buf][:, :], w0[:, 0:L], ACT.Silu).then_inc(gate_done, 1)

            def softplus_in(j):
                act.wait_ge(step_mm, j.num + 1)
                f(absx[:, :], ps_w[:, :], ACT.Abs, bias=b_dt[:, :]).then_inc(absx_done, 1)
                at_least(act, soft_done, j.num)
                f(relx[:, :], ps_w[:, :], ACT.Relu, bias=b_dt[:, :]).then_inc(relx_done, 1)

            def softplus_exp(j):
                act.wait_ge(absx_done, j.num + 1)
                at_least(act, rest_done, j.num)
                f(expx[:, :], absx[:, :], ACT.Exp, scale=-1.0).then_inc(expx_done, 1)

            def softplus_ln(j):
                act.wait_ge(expx_done, j.num + 1)
                f(lnx[:, :], expx[:, :], ACT.Ln, bias=one[:, :]).then_inc(lnx_done, 1)

            def b_high(j):
                act.wait_ge(bc_mm, j.num + 1)
                at_least(act, b_all_done, N * (j.num - 1))
                f(b_parts[j.buf][:, :], ps_w[0:SPLIT_ROWS, :], ACT.Copy).then_inc(hi_done, 1)
                at_least(act, c_stored, 16 * j.num)
                f(c_rows[C_ROW:C_ROW + N, :], ps_w[C_ROW:C_ROW + N, :], ACT.Copy).then_inc(c_rows_done, 1)

            def b_mid(j):
                act.wait_ge(b_rest_done, j.num + 1)
                f(b_parts[j.buf][0:64, :], b_rest[:, :], ACT.Copy).then_inc(mid_done, 1)

            def decays(b, n):
                if n == 0:
                    act.wait_ge(step_done, b.num + 1)
                at_least(act, scans, N * b.num + n - A_RING + 1)
                f(decay[n % A_RING][:, :, 1:L], step[b.buf][:, :].rearrange("p (d t) -> p d t", d=DIRS)[:, :, 1:L],
                  ACT.Exp, scale=a_neg[:, n:n + 1]).then_inc(decay_done, 1)

            def hid_inverse(j):
                act.wait_ge(hsum_done, j.num + 1)
                f(hln[:, :], hsum[:, :], ACT.Ln, bias=eps[:, :], scale=1.0 / C).then_inc(hln_done, 1)
                act.wait_ge(hln_done, j.num + 1)
                at_least(act, hnorm_done, j.num)
                f(hinv[:, :], hln[:, :], ACT.Exp, scale=-0.5).then_inc(hinv_done, 1)

            def out_inverse(j):
                act.wait_ge(ovar_done, j.num + 1)
                f(oln[:, :], ovar[:, :], ACT.Ln, bias=eps[:, :], scale=1.0 / C).then_inc(oln_done, 1)
                act.wait_ge(oln_done, j.num + 1)
                at_least(act, onorm_done, j.num)
                f(oinv[:, :], oln[:, :], ACT.Exp, scale=-0.5).then_inc(oinv_done, 1)

            def attend(j):
                return [lambda g=g: g(j) for g in (add_bias, softmax_exp, attn_copy, square, rms_inverse)]

            def project(j):
                return [lambda g=g: g(j) for g in (pad, conv_silu, gate_silu, softplus_in, softplus_exp,
                                                   b_high, softplus_ln, b_mid)]

            def finish(j):
                return [lambda g=g: g(j) for g in (hid_inverse, out_inverse)]

            def steps(b, done, coming, later):
                for n in range(N):
                    decays(b, n)
                    if n == 1 and coming:
                        pad(coming)
                    if n == 3 and coming:
                        conv_silu(coming)
                        gate_silu(coming)
                    if n == 6 and coming:
                        softplus_in(coming)
                        softplus_exp(coming)
                    if n == 7 and coming:
                        b_high(coming)
                    if n == 8 and coming:
                        softplus_ln(coming)
                    if n == 9 and coming:
                        b_mid(coming)
                    if n == 9 and done:
                        hid_inverse(done)
                    if n == 10 and later:
                        add_bias(later)
                    if n == 12 and later:
                        softmax_exp(later)
                    if n == 13 and done:
                        out_inverse(done)
                    if n == 14 and later:
                        attn_copy(later)
                    if n == 15 and later:
                        square(later)
                        rms_inverse(later)

            program(act, setup, attend, project, steps, finish)

        @block.gpsimd
        def _(pool):
            tt = nc.gpsimd.tensor_tensor

            def setup():
                nc.gpsimd.memset(w_bc[:, :], 0.0).then_inc(wbc_zeroed, 1)
                nc.gpsimd.memset(xpad[:, :, :], 0.0).then_inc(zeroed, 1)
                for r in range(A_RING):
                    nc.gpsimd.memset(decay[r][:, :, 0:1], 0.0).then_inc(zeroed, 1)
                pool.wait_ge(weights_ready, 1)
                

            def soft_sum(j):
                pool.wait_ge(lnx_done, j.num + 1)
                pool.wait_ge(relx_done, j.num + 1)
                at_least(pool, step_done, j.num)
                tt(absx[:, :], lnx[:, :], relx[:, :], ALU.add).then_inc(soft_done, 1)

            def soft_add(j):
                pool.wait_ge(soft_done, j.num + 1)
                pool.wait_ge(rest_done, j.num + 1)
                at_least(pool, decay_done, N * (j.num - 1))
                at_least(pool, du_done, j.num - 1)
                tt(step[j.buf][:, :], absx[:, :], rounded[:, :], ALU.add).then_inc(step_done, 1)

            def product(b, n):
                pool.wait_ge(scans, N * b.num + n + 1)
                pool.wait_ge(c_loaded[n % C_RING], 16 * ((N // C_RING) * b.num + n // C_RING + 1))
                tt(state[n % H_RING][:, :], state[n % H_RING][:, :], c_all[n % C_RING][:, :], ALU.mult
                   ).then_inc(products, 1)

            def hid_square(j):
                pool.wait_ge(hid_done, j.num + 1)
                at_least(pool, hsum_done, j.num)
                h8 = hid[:, :, :].rearrange("p d (k c) -> p (d k) c", c=C)
                tt(hidsq[:, :, :], h8, h8, ALU.mult).then_inc(hidsq_done, 1)

            def hid_norm(j):
                pool.wait_ge(hinv_done, j.num + 1)
                at_least(pool, osum_done, j.num)
                h8 = hid[:, :, :].rearrange("p d (k c) -> p (d k) c", c=C)
                tt(hnorm[:, :, :], h8, hinv[:, :].unsqueeze(2).broadcast_to([128, DIRS * CHUNKS, C]), ALU.mult
                   ).then_inc(hnorm_done, 1)

            def out_average(j):
                pool.wait_ge(osum_done, j.num + 1)
                at_least(pool, ocen_done, j.num)
                tt(oavg[:, :, :], osum[:, :, :], wf4_rows[:, :].unsqueeze(1).broadcast_to([128, CHUNKS, C]), ALU.mult
                   ).then_inc(oavg_done, 1)

            def out_square(j):
                pool.wait_ge(ocen_done, j.num + 1)
                at_least(pool, ovar_done, j.num)
                tt(osq[:, :, :], ocen[:, :, :], ocen[:, :, :], ALU.mult).then_inc(osq_done, 1)

            def out_norm(j):
                pool.wait_ge(oinv_done, j.num + 1)
                tt(onorm[:, :, :], ocen[:, :, :], oinv[:, :].unsqueeze(2).broadcast_to([128, CHUNKS, C]), ALU.mult
                   ).then_inc(onorm_done, 1)
                pool.wait_ge(onorm_done, j.num + 1)
                tt(oscaled[:, :, :], onorm[:, :, :], ln_w_rows[:, :].unsqueeze(1).broadcast_to([128, CHUNKS, C]),
                   ALU.mult).then_inc(oscaled_done, 1)
                pool.wait_ge(oscaled_done, j.num + 1)
                at_least(pool, stored, 16 * j.num)
                tt(ofin[:, :, :], oscaled[:, :, :], ln_b_rows[:, :].unsqueeze(1).broadcast_to([128, CHUNKS, C]),
                   ALU.add).then_inc(ofin_done, 1)

            def attend(j):
                return []

            def project(j):
                return [lambda g=g: g(j) for g in (soft_sum, soft_add)]

            def finish(j):
                return [lambda g=g: g(j) for g in (hid_square, hid_norm, out_average, out_square, out_norm)]

            def steps(b, done, coming, later):
                for n in range(N):
                    product(b, n)
                    if n == 5 and done:
                        hid_square(done)
                    if n == 7 and done:
                        hid_norm(done)
                    if n == 8 and coming:
                        soft_sum(coming)
                    if n == 9 and done:
                        out_average(done)
                    if n == 9 and coming:
                        soft_add(coming)
                    if n == 10 and done:
                        out_square(done)
                    if n == 12 and done:
                        out_norm(done)

            program(pool, setup, attend, project, steps, finish)

        @block.vector
        def _(dve):
            v = nc.vector

            def setup():
                v.memset(mean_w[:, :], 1.0 / C).then_inc(zeroed, 1)
                v.memset(eps[:, :], EPS).then_inc(zeroed, 1)
                v.memset(one[:, :], 1.0).then_inc(zeroed, 1)
                v.memset(w_qkv[C:, :], 0.0).then_inc(zeroed, 1)
                v.memset(w_gate[C:, :], 0.0).then_inc(zeroed, 1)
                dve.wait_ge(weights_in, 16 * N_LOADS)
                v.tensor_tensor(sigma_b[:, :], sigma[:, :], b_o2[:, :], ALU.mult)
                for tap2 in range(2):
                    v.scalar_tensor_tensor(w_conv[:, tap2, :], w_in2[:, 0:I], rms1[:, :], tap_rows[:, tap2, :],
                                           ALU.mult, ALU.mult)
                v.tensor_scalar(w_gate[0:C, :], w_in2[0:C, I:2 * I], rms1[0:C, :], None, ALU.mult)
                v.tensor_scalar(diag_d[:, :], ident[:, :], d_skip[:, :], None, ALU.mult)
                v.tensor_scalar(wf4_rows[:, :], wf_rows[:, :], 1.0 / DIRS, None, ALU.mult)
                v.tensor_copy(pick_b[:, :, :], onehot[:, :].unsqueeze(2).broadcast_to([SPLIT_ROWS, N, 128]))
                dve.wait_ge(a_exp_done, 1)
                v.tensor_scalar(a_neg[:, :], a_exp[:, :], -1.0, None, ALU.mult)
                dve.wait_ge(step_w_done, 1)
                dve.wait_ge(zeroed, A_RING + 6)
                v.tensor_copy(w_step[:, :], w0[:, 0:I]).then_inc(weights_ready, 1)
                dve.wait_ge(weights_ready, 1)

            def pool2x2(dst, src):
                v.tensor_reduce(dst.rearrange("p (h w) -> p h w", h=SIDE // 2),
                                src.rearrange("p (hh dh ww dw) -> p hh ww dh dw", hh=SIDE // 2, dh=2, dw=2),
                                AX.XY, ALU.max)

            def pooling(j):
                dve.wait_ge(qkv_done, j.num + 1)
                at_least(dve, scores_done, j.num)
                pool2x2(phi_p[:, :], w0[0:KEY, L:2 * L])
                pool2x2(g_p[:, :], w1[0:VAL, 0:L])
                v.tensor_copy(theta[:, :], w0[0:KEY, 0:L]).then_inc(pooled_done, 1)

            def row_max(j):
                dve.wait_ge(scores_done, j.num + 1)
                at_least(dve, esc_done, j.num)
                v.tensor_reduce(nmax[:, :], w0[:, 0:CHUNKS * POOLED].rearrange("p (k m) -> p k m", k=CHUNKS), AX.X,
                                ALU.max, negate=True).then_inc(nmax_done, 1)
                at_least(dve, o_done, j.num)
                v.tensor_copy(gw[:, :], w1[0:POOLED, 0:2 * C]).then_inc(gw_done, 1)

            def attn_norm(j):
                dve.wait_ge(esc_done, j.num + 1)
                v.reciprocal(erec[:, :], esum[:, :]).then_inc(erec_done, 1)
                dve.wait_ge(erec_done, j.num + 1)
                at_least(dve, attn_t_ps, j.num)
                v.tensor_tensor(attn[:, :, :], esc[:, :, :], erec[:, :].unsqueeze(2).broadcast_to([128, CHUNKS, POOLED]),
                                ALU.mult).then_inc(attn_done, 1)

            def residual(j):
                dve.wait_ge(o_done, j.num + 1)
                dve.wait_ge(xb_done, j.num + 1)
                at_least(dve, x2l_ps, j.num - 1)
                v.scalar_tensor_tensor(x2[j.buf][:, :], w1[:, 0:L], sigma[:, :], xb[:, :], ALU.mult, ALU.add
                                       ).then_inc(x2_done, 1)

            def rms(j):
                dve.wait_ge(rinv1_done, j.num + 1)
                dve.wait_ge(x2_done, j.num + 1)
                at_least(dve, gate_mm, j.num - 1)
                at_least(dve, padded, 2 * DIRS * (j.num - 1))
                v.tensor_tensor(xn[j.buf][:, :], x2[j.buf][:, :], rinv1[:, :], ALU.mult).then_inc(xn_done, 1)

            def b_low1(j):
                dve.wait_ge(hi_done, j.num + 1)
                dve.wait_ge(c_rows_done, j.num + 1)
                at_least(dve, lo_done, j.num)
                v.tensor_tensor(b_rest[:, :], ps_w[0:64, :], b_parts[j.buf][0:64, :], ALU.subtract
                                ).then_inc(b_rest_done, 1)

            def b_low2(j):
                dve.wait_ge(mid_done, j.num + 1)
                v.tensor_tensor(b_parts[j.buf][0:32, :], b_rest[0:32, :], b_parts[j.buf][0:32, :], ALU.subtract
                                ).then_inc(lo_done, 1)

            def soft_rest(j):
                dve.wait_ge(expx_done, j.num + 1)
                at_least(dve, step_done, j.num)
                v.tensor_scalar(rounded[:, :], expx[:, :], 1.0, -1.0, ALU.add, ALU.add).then_inc(rounded_done, 1)
                dve.wait_ge(rounded_done, j.num + 1)
                v.scalar_tensor_tensor(rounded[:, :], rounded[:, :], -1.0, expx[:, :], ALU.mult, ALU.add
                                       ).then_inc(rest_done, 1)

            def scan_weight(j):
                dve.wait_ge(step_done, j.num + 1)
                dve.wait_ge(u_done, j.num + 1)
                at_least(dve, input_done, N * (j.num - 1))
                v.tensor_tensor(du[j.buf][:, :], step[j.buf][:, :], u[j.buf][:, :], ALU.mult).then_inc(du_done, 1)

            def x2_copy(j):
                dve.wait_ge(x2l_ps, j.num + 1)
                v.tensor_copy(x2l[j.buf][:, :], w0[:, 0:CHUNKS * C]).then_inc(x2l_done, 1)

            def scan(b, n):
                if n == 0:
                    dve.wait_ge(du_done, b.num + 1)
                dve.wait_ge(b_all_done, N * b.num + n + 1)
                v.tensor_tensor(ps_b[n % 2][:, :], du[b.buf][:, :], ps_b[n % 2][:, :], ALU.mult
                                ).then_inc(input_done, 1)
                dve.wait_ge(input_done, N * b.num + n + 1)
                dve.wait_ge(decay_done, N * b.num + n + 1)
                at_least(dve, sums, N * b.num + n - H_RING + 1)
                v.tensor_tensor_scan(state[n % H_RING][:, :], decay[n % A_RING][:, :, :].rearrange("p d t -> p (d t)"),
                                     ps_b[n % 2][:, :], 0.0, ALU.mult, ALU.add).then_inc(scans, 1)

            def gated(j):
                dve.wait_ge(sums, N * (j.num + 1))
                dve.wait_ge(gate_done, j.num + 1)
                at_least(dve, out_mm, j.num)
                for d in range(DIRS):
                    v.tensor_tensor(grid(yg[:, d, :]), ordered(ps_y[:, L * d:L * (d + 1)], d), grid(gate[j.buf][:, :]),
                                    ALU.mult).then_inc(yg_done, 1)

            def hidden(j):
                dve.wait_ge(out_mm, j.num + 1)
                dve.wait_ge(x2l_done, j.num + 1)
                at_least(dve, hnorm_done, j.num)
                v.tensor_tensor(hid[:, :, :], w1.rearrange("p (d x) -> p d x", d=DIRS),
                                x2l[j.buf][:, :].unsqueeze(1).broadcast_to([128, DIRS, CHUNKS * C]), ALU.add
                                ).then_inc(hid_done, 1)

            def hid_sum(j):
                dve.wait_ge(hidsq_done, j.num + 1)
                at_least(dve, hln_done, j.num)
                v.tensor_reduce(hsum[:, :], hidsq[:, :, :], AX.X, ALU.add).then_inc(hsum_done, 1)

            def dir_sum(j):
                dve.wait_ge(hnorm_done, j.num + 1)
                at_least(dve, oavg_done, j.num)
                v.tensor_reduce(osum[:, :, :].rearrange("p k c -> p (k c)"),
                                hnorm[:, :, :].rearrange("p (d k) c -> p (k c) d", d=DIRS), AX.X, ALU.add
                                ).then_inc(osum_done, 1)

            def centre(j):
                dve.wait_ge(oavg_done, j.num + 1)
                v.tensor_reduce(omean[:, :], oavg[:, :, :], AX.X, ALU.add).then_inc(omean_done, 1)
                dve.wait_ge(omean_done, j.num + 1)
                at_least(dve, onorm_done, j.num)
                v.scalar_tensor_tensor(ocen[:, :, :], omean[:, :].unsqueeze(2).broadcast_to([128, CHUNKS, C]), -1.0 / C,
                                       oavg[:, :, :], ALU.mult, ALU.add).then_inc(ocen_done, 1)

            def variance(j):
                dve.wait_ge(osq_done, j.num + 1)
                at_least(dve, oln_done, j.num)
                v.tensor_reduce(ovar[:, :], osq[:, :, :], AX.X, ALU.add).then_inc(ovar_done, 1)

            def attend(j):
                return [lambda g=g: g(j) for g in (pooling, row_max, attn_norm, residual, rms)]

            def project(j):
                return [lambda g=g: g(j) for g in (b_low1, soft_rest, b_low2, x2_copy, scan_weight)]

            def finish(j):
                return [lambda g=g: g(j) for g in (gated, hidden, hid_sum, dir_sum, centre, variance)]

            def steps(b, done, coming, later):
                for n in range(N):
                    scan(b, n)
                    if n == 2 and done:
                        gated(done)
                    if n == 3 and done:
                        hidden(done)
                    if n == 6 and coming:
                        b_low1(coming)
                        soft_rest(coming)
                    if n == 6 and done:
                        hid_sum(done)
                    if n == 7 and coming:
                        b_low2(coming)
                        x2_copy(coming)
                    if n == 8 and done:
                        dir_sum(done)
                    if n == 9 and done:
                        centre(done)
                    if n == 9 and later:
                        pooling(later)
                    if n == 10 and coming:
                        scan_weight(coming)
                    if n == 10 and later:
                        row_max(later)
                    if n == 11 and done:
                        variance(done)
                    if n == 11 and later:
                        attn_norm(later)
                    if n == 13 and later:
                        residual(later)
                    if n == 15 and later:
                        rms(later)

            program(dve, setup, attend, project, steps, finish)


def kernel(x, L0_conv_w_theta, L0_conv_w_phi, L0_conv_w_g, L0_conv_w_o, L0_conv_b_o, L0_conv_sigma, L1_conv_W_in,
           L1_conv_conv_w, L1_conv_conv_b, L1_conv_W_x, L1_conv_W_dt, L1_conv_b_dt, L1_conv_A_log, L1_conv_Dp,
           L1_conv_W_out, L1_conv_rms_w1, L1_conv_rms_wf, L1_conv_ln_w, L1_conv_ln_b):
    import numpy as np
    import concourse.bacc as bacc
    from concourse.bass_utils import run_bass_kernel_spmd

    x = np.asarray(x)
    arrays = {
        "x_t": x.reshape(IMAGES, L, C).transpose(0, 2, 1),
        "w_theta": L0_conv_w_theta, "w_phi": L0_conv_w_phi, "w_g": L0_conv_w_g, "w_o": L0_conv_w_o,
        "b_o": L0_conv_b_o, "sigma": np.asarray(L0_conv_sigma).reshape(1),
        "w_in_t": np.asarray(L1_conv_W_in).T, "conv_w_t": np.asarray(L1_conv_conv_w).reshape(I, TAPS).T,
        "conv_b": L1_conv_conv_b, "W_x": L1_conv_W_x, "w_x_t": np.asarray(L1_conv_W_x).T,
        "w_dt_t": np.asarray(L1_conv_W_dt).T, "b_dt": L1_conv_b_dt, "A_log": L1_conv_A_log, "Dp": L1_conv_Dp,
        "w_out_t": np.asarray(L1_conv_W_out).T, "rms_w1": L1_conv_rms_w1, "rms_wf": L1_conv_rms_wf,
        "ln_w": L1_conv_ln_w, "ln_b": L1_conv_ln_b,
        "ident": np.eye(128, dtype=np.float32),
        "onehot": np.tile(np.eye(32, N, dtype=np.float32), (COPIES, 1)),
    }
    arrays = {name: np.ascontiguousarray(v) for name, v in arrays.items()}
    nc = bacc.Bacc("TRN2", target_bir_lowering=False, num_devices=1)
    aps = {name: nc.dram_tensor(f"in_{name}", v.shape, mybir.dt.from_np(v.dtype), kind="ExternalInput").ap()
           for name, v in arrays.items()}
    out = nc.dram_tensor("out", (IMAGES, L, C), F32, kind="ExternalOutput").ap()
    build(nc, aps, out)
    r = run_bass_kernel_spmd(nc, [{f"in_{name}": v for name, v in arrays.items()}], core_ids=[0])
    return r.results[0]["out"].reshape(IMAGES, SIDE, SIDE, C)
```

```python
import concourse.bass as bass
from concourse import mybir
from contextlib import ExitStack

F32 = mybir.dt.float32
BF16 = mybir.dt.bfloat16
ALU = mybir.AluOpType
ACT = mybir.ActivationFunctionType
AX = mybir.AxisListType

IMAGES, SIDE, C = 16, 16, 64
L = SIDE * SIDE
POOLED = L // 4
KEY, VAL = C // 8, C // 2
I = 2 * C
N = 16
R = 16
TAPS = 4
DIRS = 4
T = DIRS * L
HALF = T // 2
CHUNKS = L // 128
PADDED = L + 4
EPS = 1e-5
COPIES = 3
SPLIT_ROWS = 32 * COPIES
C_ROW = SPLIT_ROWS
A_RING, H_RING, C_RING = 4, 8, 4
SUM_BEFORE = {6: (1,), 8: (3,), 9: (4,), 13: (8, 9), 15: (12,)}
SUM_AFTER = {2: (0,), 6: (2,), 9: (5,), 10: (6,), 11: (7,), 13: (10,), 14: (11,)}
SUM_NEXT = {0: (13,), 1: (14, 15)}
EXP_LN, SILU = "natural_log_exp_and_others", "silu_and_others"
THETA, PHI, G = 0, 32, 64


class Image:

    def __init__(self, pair, offset):
        self.pair, self.offset = pair, offset
        self.num = 2 * pair + offset
        self.buf = offset % 2

    def __add__(self, d):
        return Image(self.pair, self.offset + d)


def at_least(eng, sem, value):
    if not isinstance(value, int) or value > 0:
        eng.wait_ge(sem, value)


def all_at_least(eng, *waits):
    values = [v if isinstance(v, int) else eng.snap(eng.to_reg(v)) for _, v in waits]
    for (sem, _), value in zip(waits, values):
        at_least(eng, sem, value)


def build(nc, a, out):
    ctx = ExitStack()
    with ctx:
        def sb(name, shape, dt=F32):
            return ctx.enter_context(nc.sbuf_tensor(name, shape, dt))

        def ps(name, shape):
            return ctx.enter_context(nc.psum_tensor(name, shape, F32))

        def sem(name):
            return ctx.enter_context(nc.semaphore(name))

        ident = sb("ident", [128, 128])
        w_qkv = sb("w_qkv", [2 * C, 128])
        w_o2 = sb("w_o2", [VAL, 2 * C])
        sigma = sb("sigma", [128, 1])
        b_o2 = sb("b_o2", [128, 1])
        sigma_b = sb("sigma_b", [128, 1])
        w_in2 = sb("w_in2", [128, 2 * I])
        rms1 = sb("rms1", [128, 1])
        tap_rows = sb("tap_rows", [128, 2, I])
        w_conv = sb("w_conv", [128, 2, I])
        w_gate = sb("w_gate", [2 * C, I])
        conv_b = sb("conv_b", [I, 1])
        b_dt = sb("b_dt", [I, 1])
        d_skip = sb("d_skip", [I, 1])
        diag_d = sb("diag_d", [I, I])
        a_log = sb("a_log", [I, N])
        a_exp = sb("a_exp", [I, N])
        a_neg = sb("a_neg", [I, N])
        w_bc = sb("w_bc", [I, C_ROW + N])
        w_x_dt = sb("w_x_dt", [R, I])
        w_dt = sb("w_dt", [R, I])
        w_step = sb("w_step", [I, I])
        w_out = sb("w_out", [I, C])
        wf_rows = sb("wf_rows", [128, C])
        wf4_rows = sb("wf4_rows", [128, C])
        ln_w_rows = sb("ln_w_rows", [128, C])
        ln_b_rows = sb("ln_b_rows", [128, C])
        mean_w = sb("mean_w", [C, 128])
        eps = sb("eps", [128, 1])
        one = sb("one", [128, 1])
        onehot = sb("onehot", [SPLIT_ROWS, N])
        neg_ident = sb("neg_ident", [128, 128], BF16)
        pick_b = sb("pick_b", [SPLIT_ROWS, N, 128], BF16)

        xt = sb("xt", [128, L])
        xb = sb("xb", [128, L])
        theta = sb("theta", [KEY, L])
        phi_p = sb("phi_p", [KEY, POOLED])
        g_p = sb("g_p", [VAL, POOLED])
        gw = sb("gw", [POOLED, 2 * C])
        nmax = sb("nmax", [128, CHUNKS])
        esc = sb("esc", [128, CHUNKS, POOLED])
        esum = sb("esum", [128, CHUNKS])
        erec = sb("erec", [128, CHUNKS])
        attn = sb("attn", [128, CHUNKS, POOLED])
        attn_t = sb("attn_t", [POOLED, L])
        x2 = [sb(f"x2_{q}", [128, L]) for q in range(2)]
        x2sq = sb("x2sq", [C, L])
        ln1 = sb("ln1", [128, L])
        rinv1 = sb("rinv1", [128, L])
        xn = [sb(f"xn_{q}", [128, L]) for q in range(2)]
        xpad = sb("xpad", [128, DIRS, PADDED])
        u = [sb(f"u_{q}", [I, T]) for q in range(2)]
        gate = [sb(f"gate_{q}", [I, L]) for q in range(2)]
        x2l = [sb(f"x2l_{q}", [128, CHUNKS * C]) for q in range(2)]
        absx = sb("absx", [I, T])
        relx = sb("relx", [I, T])
        expx = sb("expx", [I, T])
        onex = sb("onex", [I, T])
        lnx = sb("lnx", [I, T])
        lost = sb("lost", [I, T])
        soft = sb("soft", [I, T])
        step = [sb(f"step_{q}", [I, T]) for q in range(2)]
        du = [sb(f"du_{q}", [I, T]) for q in range(2)]
        b_parts = [sb(f"b_parts_{q}", [SPLIT_ROWS, T], BF16) for q in range(2)]
        c_rows = sb("c_rows", [128, T])
        decay = [sb(f"decay_{r}", [I, DIRS, L]) for r in range(A_RING)]
        state = [sb(f"state_{r}", [I, T]) for r in range(H_RING)]
        c_all = [sb(f"c_all_{r}", [I, T]) for r in range(C_RING)]
        yg = sb("yg", [I, DIRS, L])
        hid = sb("hid", [128, DIRS, CHUNKS * C])
        hidsq = sb("hidsq", [128, DIRS * CHUNKS, C])
        hsum = sb("hsum", [128, DIRS * CHUNKS])
        hln = sb("hln", [128, DIRS * CHUNKS])
        hinv = sb("hinv", [128, DIRS * CHUNKS])
        hnorm = sb("hnorm", [128, DIRS * CHUNKS, C])
        osum = sb("osum", [128, CHUNKS, C])
        oavg = sb("oavg", [128, CHUNKS, C])
        omean = sb("omean", [128, CHUNKS])
        ocen = sb("ocen", [128, CHUNKS, C])
        osq = sb("osq", [128, CHUNKS, C])
        ovar = sb("ovar", [128, CHUNKS])
        oln = sb("oln", [128, CHUNKS])
        oinv = sb("oinv", [128, CHUNKS])
        onorm = sb("onorm", [128, CHUNKS, C])
        oscaled = sb("oscaled", [128, CHUNKS, C])
        ofin = sb("ofin", [128, CHUNKS, C])

        ps_b = [ps(f"ps_b{q}", [128, T]) for q in range(2)]
        ps_y = ps("ps_y", [128, T])
        ps_w = ps("ps_w", [128, T])
        w0, w1 = ps_w[:, 0:HALF], ps_w[:, HALF:T]

        c_dram = [nc.dram_tensor(f"c_dram_{q}", [N, T], F32, kind="Internal").ap() for q in range(2)]

        weights_in = sem("weights_in")
        zeroed = sem("zeroed")
        gaps_zeroed = sem("gaps_zeroed")
        a_exp_done = sem("a_exp_done")
        step_w_done = sem("step_w_done")
        weights_ready = sem("weights_ready")
        x_loaded = sem("x_loaded")
        xb_done = sem("xb_done")
        qkv_done = sem("qkv_done")
        pooled_done = sem("pooled_done")
        scores_done = sem("scores_done")
        nmax_done = sem("nmax_done")
        gw_done = sem("gw_done")
        esc_done = sem("esc_done")
        erec_done = sem("erec_done")
        attn_done = sem("attn_done")
        attn_t_ps = sem("attn_t_ps")
        attn_t_done = sem("attn_t_done")
        o_done = sem("o_done")
        x2_done = sem("x2_done")
        x2sq_done = sem("x2sq_done")
        ms_done = sem("ms_done")
        ln1_done = sem("ln1_done")
        rinv1_done = sem("rinv1_done")
        xn_done = sem("xn_done")
        padded = sem("padded")
        conv_done = sem("conv_done")
        u_done = sem("u_done")
        gate_mm = sem("gate_mm")
        gate_done = sem("gate_done")
        step_mm = sem("step_mm")
        absx_done = sem("absx_done")
        relx_done = sem("relx_done")
        expx_done = sem("expx_done")
        lnx_done = sem("lnx_done")
        onex_done = sem("onex_done")
        rest_done = sem("rest_done")
        soft_done = sem("soft_done")
        step_done = sem("step_done")
        du_done = sem("du_done")
        bc_mm = sem("bc_mm")
        hi_done = sem("hi_done")
        c_rows_done = sem("c_rows_done")
        rest1_mm = sem("rest1_mm")
        rest2_mm = sem("rest2_mm")
        mid_done = sem("mid_done")
        lo_done = sem("lo_done")
        c_stored = sem("c_stored")
        x2l_ps = sem("x2l_ps")
        x2l_done = sem("x2l_done")
        decay_done = sem("decay_done")
        b_all_done = sem("b_all_done")
        input_done = sem("input_done")
        scans = sem("scans")
        c_loaded = [sem(f"c_loaded{r}") for r in range(C_RING)]
        products = sem("products")
        sums = sem("sums")
        yg_done = sem("yg_done")
        out_mm = sem("out_mm")
        hid_done = sem("hid_done")
        hsum_done = sem("hsum_done")
        hln_done = sem("hln_done")
        hinv_done = sem("hinv_done")
        hnorm_done = sem("hnorm_done")
        osum_done = sem("osum_done")
        oavg_done = sem("oavg_done")
        omean_done = sem("omean_done")
        ocen_done = sem("ocen_done")
        osq_done = sem("osq_done")
        ovar_done = sem("ovar_done")
        oln_done = sem("oln_done")
        oinv_done = sem("oinv_done")
        onorm_done = sem("onorm_done")
        oscaled_done = sem("oscaled_done")
        ofin_done = sem("ofin_done")
        stored = sem("stored")

        def ordered(view, d):
            v = view.rearrange("p (h w) -> p h w", h=SIDE)
            if d in (2, 3):
                v = v[:, ::-1, :]
            if d in (1, 3):
                v = v[:, :, ::-1]
            return v

        def grid(view):
            return view.rearrange("p (h w) -> p h w", h=SIDE)

        column = lambda v: v.rearrange("(p a) -> p a", a=1)
        loads = [
            (ident[:, :], a["ident"]),
            (w_o2[:, 0:C], a["w_o"]),
            (w_o2[:, C:], a["w_o"]),
            (sigma[:, :], a["sigma"].partition_broadcast(128)),
            (b_o2[0:C, :], column(a["b_o"])),
            (b_o2[C:, :], column(a["b_o"])),
            (w_in2[0:C, :], a["w_in_t"]),
            (w_in2[C:, :], a["w_in_t"]),
            (rms1[0:C, :], column(a["rms_w1"])),
            (rms1[C:, :], column(a["rms_w1"])),
            (tap_rows[0:C, 0, :], a["conv_w_t"][0, :].partition_broadcast(C)),
            (tap_rows[C:, 0, :], a["conv_w_t"][1, :].partition_broadcast(C)),
            (tap_rows[0:C, 1, :], a["conv_w_t"][2, :].partition_broadcast(C)),
            (tap_rows[C:, 1, :], a["conv_w_t"][3, :].partition_broadcast(C)),
            (conv_b[:, :], column(a["conv_b"])),
            (b_dt[:, :], column(a["b_dt"])),
            (d_skip[:, :], column(a["Dp"])),
            (a_log[:, :], a["A_log"]),
            (w_x_dt[:, :], a["W_x"][0:R, :]),
            (w_dt[:, :], a["w_dt_t"]),
            (w_out[:, :], a["w_out_t"]),
            (wf_rows[:, :], a["rms_wf"].partition_broadcast(128)),
            (ln_w_rows[:, :], a["ln_w"].partition_broadcast(128)),
            (ln_b_rows[:, :], a["ln_b"].partition_broadcast(128)),
            (onehot[:, :], a["onehot"]),
        ]
        gapped_loads = [(w_bc[:, 32 * k:32 * k + N], a["w_x_t"][:, R:R + N]) for k in range(COPIES)]
        gapped_loads.append((w_bc[:, C_ROW:C_ROW + N], a["w_x_t"][:, R + N:]))
        gapped_loads += [(w_qkv[0:C, THETA:THETA + KEY], a["w_theta"]), (w_qkv[0:C, PHI:PHI + KEY], a["w_phi"]),
                       (w_qkv[0:C, G:G + VAL], a["w_g"])]
        N_LOADS = len(loads) + len(gapped_loads)

        block = ctx.enter_context(nc.Block())

        def program(eng, setup, attend, project, steps, finish):
            setup()
            first = Image(0, 0)
            for part in attend(first):
                part()
            for part in project(first):
                part()
            for part in attend(first + 1):
                part()
            steps(first, None, first + 1, first + 2)
            steps(first + 1, first, first + 2, first + 3)
            with eng.Fori(0, (IMAGES - 4) // 2) as pair:
                for offset in (2, 3):
                    b = Image(pair, offset)
                    steps(b, b + -1, b + 1, b + 2)
            last = Image(0, IMAGES - 1)
            steps(last + -1, last + -2, last, None)
            steps(last, last + -1, None, None)
            for part in finish(last):
                part()

        @block.sync
        def _(sp):
            def setup():
                for dst, src in loads:
                    sp.dma_start(dst, src).then_inc(weights_in, 16)
                sp.wait_ge(gaps_zeroed, 2)
                for dst, src in gapped_loads:
                    sp.dma_start(dst, src).then_inc(weights_in, 16)

            def load_x(j):
                all_at_least(sp, (xb_done, j.num), (qkv_done, j.num))
                sp.wait_ge(weights_ready, 1)
                for half in range(2):
                    sp.dma_start(xt[C * half:C * half + C, :], a["x_t"][j.num, :, :]).then_inc(x_loaded, 16)

            def store_c(j):
                all_at_least(sp, (c_rows_done, j.num + 1), (products, N * (j.num - 1)))
                sp.dma_start(c_dram[j.buf], c_rows[C_ROW:C_ROW + N, :]).then_inc(c_stored, 16)

            def load_c(b, n):
                stored_c = [(c_stored, 16 * (b.num + 1))] if n == 0 else []
                all_at_least(sp, *stored_c, (products, N * b.num + n - C_RING + 1))
                sp.dma_start(c_all[n % C_RING][:, :], c_dram[b.buf][n, :].partition_broadcast(128)
                             ).then_inc(c_loaded[n % C_RING], 16)

            def store_out(j):
                sp.wait_ge(ofin_done, j.num + 1)
                sp.wait_ge(weights_ready, 1)
                sp.dma_start(out[j.num, :, :].rearrange("(k p) c -> p k c", p=128), ofin[:, :, :]
                             ).then_inc(stored, 16)

            def attend(j):
                return [lambda: load_x(j)]

            def project(j):
                return [lambda: store_c(j)]

            def finish(j):
                return [lambda: store_out(j)]

            def steps(b, done, coming, later):
                for n in range(N):
                    load_c(b, n)
                    if n == 8 and later:
                        load_x(later)
                    if n == 15 and coming:
                        store_c(coming)
                    if n == 15 and done:
                        store_out(done)

            program(sp, setup, attend, project, steps, finish)
            sp.wait_ge(stored, 16 * IMAGES)

        @block.tensor
        def _(pe):
            mm = nc.tensor.matmul

            def setup():
                pe.wait_ge(weights_in, 16 * N_LOADS)
                mm(w0[:, 0:I], w_x_dt[:, :], w_dt[:, :], start=True, stop=True).then_inc(step_w_done, 1)
                pe.wait_ge(weights_ready, 1)

            def qkv(j):
                pe.wait_ge(x_loaded, 32 * (j.num + 1))
                at_least(pe, c_rows_done, j.num)
                mm(w0[:, 0:L], w_qkv[:, :], xt[:, :], start=True, stop=True).then_inc(qkv_done, 1)

            def scores(j):
                pe.wait_ge(pooled_done, j.num + 1)
                for k in range(CHUNKS):
                    mm(w0[:, POOLED * k:POOLED * (k + 1)], theta[:, 128 * k:128 * (k + 1)], phi_p[:, :],
                       start=True, stop=True)
                mm(w0[0:POOLED, 2 * C:4 * C], g_p[:, :], w_o2[:, :], start=True, stop=True
                   ).then_inc(scores_done, 1)

            def attn_turn(j):
                pe.wait_ge(attn_done, j.num + 1)
                pe.wait_ge(gw_done, j.num + 1)
                for k in range(CHUNKS):
                    last = mm(w0[0:POOLED, 128 * k:128 * (k + 1)], attn[:, k, :], ident[:, :], start=True, stop=True)
                last.then_inc(attn_t_ps, 1)

            def attn_out(j):
                pe.wait_ge(attn_t_done, j.num + 1)
                pe.wait_ge(gw_done, j.num + 1)
                mm(w0[:, L:2 * L], gw[:, :], attn_t[:, :], start=True, stop=True).then_inc(o_done, 1)

            def x2_turn(j):
                pe.wait_ge(x2_done, j.num + 1)
                at_least(pe, hid_done, j.num - 1)
                for k in range(CHUNKS):
                    last = mm(w1[:, C * k:C * (k + 1)], x2[j.buf][0:C, 128 * k:128 * (k + 1)], ident[0:C, 0:C],
                              start=True, stop=True)
                last.then_inc(x2l_ps, 1)

            def mean_square(j):
                pe.wait_ge(x2sq_done, j.num + 1)
                mm(w0[:, 0:L], mean_w[:, :], x2sq[:, :], start=True, stop=True).then_inc(ms_done, 1)

            def conv(j, half, tap2):
                if tap2 == 0:
                    pe.wait_ge(padded, 2 * DIRS * j.num + DIRS * (half + 1))
                    if half == 1:
                        pe.wait_ge(x2l_done, j.num + 1)
                mm(ps_w[:, HALF * half:HALF * (half + 1)], w_conv[:, tap2, :],
                   xpad[:, 2 * half:2 * half + 2, 2 * tap2:2 * tap2 + L],
                   start=(tap2 == 0), stop=(tap2 == 1)).then_inc(conv_done, 1)

            def gate_proj(j):
                pe.wait_ge(u_done, 2 * j.num + 1)
                mm(w0[:, 0:L], w_gate[:, :], xn[j.buf][:, :], start=True, stop=True).then_inc(gate_mm, 1)

            def step_proj(j):
                pe.wait_ge(gate_done, j.num + 1)
                pe.wait_ge(u_done, 2 * (j.num + 1))
                for half in range(2):
                    last = mm(ps_w[:, HALF * half:HALF * (half + 1)], w_step[:, :],
                              u[j.buf][:, HALF * half:HALF * (half + 1)], start=True, stop=True)
                last.then_inc(step_mm, 1)

            def bc_proj(j, half):
                pe.wait_ge(relx_done, j.num + 1)
                mm(ps_w[0:C_ROW + N, HALF * half:HALF * (half + 1)], w_bc[:, :],
                   u[j.buf][:, HALF * half:HALF * (half + 1)], start=True, stop=True).then_inc(bc_mm, 1)

            def b_rest(j, level):
                rows = 32 * (COPIES - level)
                pe.wait_ge(hi_done if level == 1 else mid_done, j.num + 1)
                for half in range(2):
                    last = mm(ps_w[0:rows, HALF * half:HALF * (half + 1)], neg_ident[0:SPLIT_ROWS, 0:rows],
                              b_parts[j.buf][:, HALF * half:HALF * (half + 1)], start=False, stop=True,
                              skip_group_check=True)
                last.then_inc(rest1_mm if level == 1 else rest2_mm, 1)

            def out_proj(j):
                pe.wait_ge(yg_done, DIRS * (j.num + 1))
                if j.offset < IMAGES - 1:
                    pe.wait_ge(c_rows_done, j.num + 2)
                at_least(pe, hid_done, j.num)
                for d in range(DIRS):
                    for k in range(CHUNKS):
                        m = CHUNKS * d + k
                        last = mm(w1[:, C * m:C * (m + 1)], yg[:, d, 128 * k:128 * (k + 1)], w_out[:, :],
                                  start=True, stop=True)
                last.then_inc(out_mm, 1)

            def spread_b(b, n):
                if n == 0:
                    pe.wait_ge(lo_done, b.num + 1)
                at_least(pe, scans, N * b.num + n - 1)
                for half in range(2):
                    last = mm(ps_b[n % 2][:, HALF * half:HALF * (half + 1)], pick_b[:, n, :],
                              b_parts[b.buf][:, HALF * half:HALF * (half + 1)], start=True, stop=True)
                last.then_inc(b_all_done, 1)

            def skip(b, half):
                mm(ps_y[:, HALF * half:HALF * (half + 1)], diag_d[:, :],
                   u[b.buf][:, HALF * half:HALF * (half + 1)], start=False, stop=False)

            def sum_state(b, n):
                pe.wait_ge(products, N * b.num + n + 1)
                if n == 0:
                    at_least(pe, yg_done, DIRS * b.num)
                for half in range(2):
                    last = mm(ps_y[:, HALF * half:HALF * (half + 1)], ident[:, :],
                              state[n % H_RING][:, HALF * half:HALF * (half + 1)],
                              start=(n == 0), stop=(n == N - 1))
                last.then_inc(sums, 1)

            def attend(j):
                parts = [lambda g=g: g(j) for g in (qkv, scores, attn_turn, attn_out)]
                return parts if j.offset == 0 else [lambda: spread_b(j + -1, 0)] + parts

            def project(j):
                return [lambda: mean_square(j), lambda: x2_turn(j),
                        lambda: conv(j, 0, 0), lambda: conv(j, 0, 1), lambda: conv(j, 1, 0), lambda: conv(j, 1, 1),
                        lambda: gate_proj(j), lambda: step_proj(j), lambda: bc_proj(j, 0), lambda: bc_proj(j, 1),
                        lambda: b_rest(j, 1), lambda: b_rest(j, 2)]

            def finish(j):
                return [lambda k=k: sum_state(j, k) for n in (0, 1) for k in SUM_NEXT[n]] + [lambda: out_proj(j)]

            def steps(b, done, coming, later):
                for n in range(N):
                    if done:
                        for k in SUM_NEXT.get(n, ()):
                            sum_state(done, k)
                    for k in SUM_BEFORE.get(n, ()):
                        sum_state(b, k)
                    if n == 0 and coming:
                        mean_square(coming)
                    if n == 1 and coming:
                        conv(coming, 0, 0)
                    if n == 2 and done:
                        out_proj(done)
                    if n == 3 and coming:
                        x2_turn(coming)
                        conv(coming, 0, 1)
                    if n == 4 and coming:
                        conv(coming, 1, 0)
                    if n == 5 and coming:
                        gate_proj(coming)
                    if n == 6 and coming:
                        step_proj(coming)
                    if n in (8, 9) and coming:
                        bc_proj(coming, n - 8)
                    if n == 11 and coming:
                        b_rest(coming, 2)
                    if n == 13 and later:
                        scores(later)

                    if n < N - 1:
                        spread_b(b, n + 1)

                    for k in SUM_AFTER.get(n, ()):
                        sum_state(b, k)
                    if n == 3:
                        skip(b, 0)
                    if n == 4 and coming:
                        conv(coming, 1, 1)
                    if n == 9 and coming:
                        b_rest(coming, 1)
                    if n == 12 and later:
                        qkv(later)
                    if n == 13:
                        skip(b, 1)
                    if n == 14 and later:
                        attn_turn(later)
                    if n == 15 and later:
                        attn_out(later)
                    if n == 15 and coming:
                        spread_b(coming, 0)

            program(pe, setup, attend, project, steps, finish)

        @block.scalar
        def _(act):
            f = nc.scalar.activation

            def setup():
                act.wait_ge(weights_in, 16 * N_LOADS)
                act.preload_act_table_set(EXP_LN)
                f(a_exp[:, :], a_log[:, :], ACT.Exp).then_inc(a_exp_done, 1)
                act.wait_ge(weights_ready, 1)

            def add_bias(j):
                act.wait_ge(x_loaded, 32 * (j.num + 1))
                at_least(act, x2_done, j.num)
                f(xb[:, :], xt[:, :], ACT.Identity, bias=sigma_b[:, :]).then_inc(xb_done, 1)

            def softmax_exp(j):
                act.wait_ge(nmax_done, j.num + 1)
                at_least(act, attn_done, j.num)
                for k in range(CHUNKS):
                    last = f(esc[:, k, :], w0[:, POOLED * k:POOLED * (k + 1)], ACT.Exp, bias=nmax[:, k:k + 1],
                             accum_out=esum[:, k:k + 1])
                last.then_inc(esc_done, 1)

            def attn_copy(j):
                act.wait_ge(attn_t_ps, j.num + 1)
                at_least(act, o_done, j.num)
                f(attn_t[:, :], w0[0:POOLED, 0:L], ACT.Copy).then_inc(attn_t_done, 1)

            def square(j):
                act.wait_ge(x2_done, j.num + 1)
                at_least(act, ms_done, j.num)
                f(x2sq[:, :], x2[j.buf][0:C, :], ACT.Square).then_inc(x2sq_done, 1)

            def rms_inverse(j):
                act.wait_ge(ms_done, j.num + 1)
                f(ln1[:, :], w0[:, 0:L], ACT.Ln, bias=eps[:, :]).then_inc(ln1_done, 1)
                at_least(act, xn_done, j.num)
                act.wait_ge(ln1_done, j.num + 1)
                f(rinv1[:, :], ln1[:, :], ACT.Exp, scale=-0.5).then_inc(rinv1_done, 1)

            def pad(j):
                act.wait_ge(xn_done, j.num + 1)
                at_least(act, conv_done, 4 * j.num)
                for d in range(DIRS):
                    f(grid(xpad[0:C, d, 3:3 + L]), ordered(xn[j.buf][0:C, :], d), ACT.Copy).then_inc(padded, 1)
                    f(grid(xpad[C:, d, 2:2 + L]), ordered(xn[j.buf][C:, :], d), ACT.Copy).then_inc(padded, 1)

            def conv_silu(j):
                act.preload_act_table_set(SILU)
                act.wait_ge(conv_done, 4 * j.num + 2)
                at_least(act, sums, N * (j.num - 1))
                at_least(act, du_done, j.num - 1)
                f(u[j.buf][:, 0:HALF], w0, ACT.Silu, bias=conv_b[:, :]).then_inc(u_done, 1)
                act.wait_ge(conv_done, 4 * (j.num + 1))
                f(u[j.buf][:, HALF:T], w1, ACT.Silu, bias=conv_b[:, :]).then_inc(u_done, 1)

            def gate_silu(j):
                act.wait_ge(gate_mm, j.num + 1)
                at_least(act, yg_done, DIRS * (j.num - 1))
                f(gate[j.buf][:, :], w0[:, 0:L], ACT.Silu).then_inc(gate_done, 1)
                act.preload_act_table_set(EXP_LN)

            def softplus_in(j):
                act.wait_ge(step_mm, j.num + 1)
                f(absx[:, :], ps_w[:, :], ACT.Abs, bias=b_dt[:, :]).then_inc(absx_done, 1)
                at_least(act, soft_done, j.num)
                f(relx[:, :], ps_w[:, :], ACT.Relu, bias=b_dt[:, :]).then_inc(relx_done, 1)

            def softplus_exp(j):
                act.wait_ge(absx_done, j.num + 1)
                at_least(act, rest_done, j.num)
                f(expx[:, :], absx[:, :], ACT.Exp, scale=-1.0).then_inc(expx_done, 1)
                act.wait_ge(expx_done, j.num + 1)
                f(onex[:, :], expx[:, :], ACT.Identity, bias=one[:, :]).then_inc(onex_done, 1)

            def softplus_ln(j):
                act.wait_ge(onex_done, j.num + 1)
                f(lnx[:, :], onex[:, :], ACT.Ln).then_inc(lnx_done, 1)

            def b_hi(j):
                act.wait_ge(bc_mm, 2 * (j.num + 1))
                at_least(act, b_all_done, N * (j.num - 1))
                f(b_parts[j.buf][:, :], ps_w[0:SPLIT_ROWS, :], ACT.Copy).then_inc(hi_done, 1)

            def c_copy(j):
                act.wait_ge(bc_mm, 2 * (j.num + 1))
                at_least(act, c_stored, 16 * j.num)
                f(c_rows[C_ROW:C_ROW + N, :], ps_w[C_ROW:C_ROW + N, :], ACT.Copy).then_inc(c_rows_done, 1)

            def b_mid(j):
                act.wait_ge(rest1_mm, j.num + 1)
                f(b_parts[j.buf][0:64, :], ps_w[0:64, :], ACT.Copy).then_inc(mid_done, 1)

            def b_lo(j):
                act.wait_ge(rest2_mm, j.num + 1)
                f(b_parts[j.buf][0:32, :], ps_w[0:32, :], ACT.Copy).then_inc(lo_done, 1)

            def decays(b, n):
                if n == 0:
                    act.wait_ge(step_done, b.num + 1)
                at_least(act, scans, N * b.num + n - A_RING + 1)
                f(decay[n % A_RING][:, :, 1:L], step[b.buf][:, :].rearrange("p (d t) -> p d t", d=DIRS)[:, :, 1:L],
                  ACT.Exp, scale=a_neg[:, n:n + 1]).then_inc(decay_done, 1)

            def hid_inverse(j):
                act.wait_ge(hid_done, j.num + 1)
                at_least(act, hln_done, j.num)
                for d in range(DIRS):
                    for k in range(CHUNKS):
                        m = CHUNKS * d + k
                        last = f(hidsq[:, m, :], hid[:, d, C * k:C * (k + 1)], ACT.Square, accum_out=hsum[:, m:m + 1])
                last.then_inc(hsum_done, 1)
                act.wait_ge(hsum_done, j.num + 1)
                f(hln[:, :], hsum[:, :], ACT.Ln, bias=eps[:, :], scale=1.0 / C).then_inc(hln_done, 1)
                act.wait_ge(hln_done, j.num + 1)
                at_least(act, hnorm_done, j.num)
                f(hinv[:, :], hln[:, :], ACT.Exp, scale=-0.5).then_inc(hinv_done, 1)

            def out_inverse(j):
                act.wait_ge(ovar_done, j.num + 1)
                f(oln[:, :], ovar[:, :], ACT.Ln, bias=eps[:, :], scale=1.0 / C).then_inc(oln_done, 1)
                act.wait_ge(oln_done, j.num + 1)
                at_least(act, onorm_done, j.num)
                f(oinv[:, :], oln[:, :], ACT.Exp, scale=-0.5).then_inc(oinv_done, 1)

            def attend(j):
                return []

            def project(j):
                return [lambda g=g: g(j) for g in (
                    add_bias, softmax_exp, attn_copy, square, rms_inverse, pad, conv_silu, gate_silu, softplus_in,
                    softplus_exp, b_hi, softplus_ln, b_mid, b_lo, c_copy)]

            def finish(j):
                return [lambda g=g: g(j) for g in (hid_inverse, out_inverse)]

            def steps(b, done, coming, later):
                for n in range(N):
                    decays(b, n)
                    if n == 1 and coming:
                        add_bias(coming)
                        softmax_exp(coming)
                    if n == 2 and coming:
                        attn_copy(coming)
                        square(coming)
                        rms_inverse(coming)
                    if n == 3 and coming:
                        pad(coming)
                    if n == 6 and done:
                        hid_inverse(done)
                    if n == 6 and coming:
                        conv_silu(coming)
                        gate_silu(coming)
                    if n == 7 and coming:
                        softplus_in(coming)
                    if n == 8 and coming:
                        softplus_exp(coming)
                    if n == 11 and coming:
                        b_hi(coming)
                        softplus_ln(coming)
                    if n == 13 and coming:
                        b_mid(coming)
                    if n == 14 and coming:
                        b_lo(coming)
                        c_copy(coming)
                    if n == 15 and done:
                        out_inverse(done)

            program(act, setup, attend, project, steps, finish)

        @block.gpsimd
        def _(pool):
            tt = nc.gpsimd.tensor_tensor

            def setup():
                nc.gpsimd.memset(w_bc[:, :], 0.0).then_inc(gaps_zeroed, 1)
                nc.gpsimd.memset(xpad[:, :, :], 0.0).then_inc(zeroed, 1)
                for r in range(A_RING):
                    nc.gpsimd.memset(decay[r][:, :, 0:1], 0.0).then_inc(zeroed, 1)
                pool.wait_ge(weights_ready, 1)
                

            def soft_sum(j):
                pool.wait_ge(lnx_done, j.num + 1)
                pool.wait_ge(relx_done, j.num + 1)
                at_least(pool, step_done, j.num)
                tt(soft[:, :], lnx[:, :], relx[:, :], ALU.add).then_inc(soft_done, 1)

            def soft_add(j):
                pool.wait_ge(soft_done, j.num + 1)
                pool.wait_ge(rest_done, j.num + 1)
                at_least(pool, decay_done, N * (j.num - 1))
                at_least(pool, du_done, j.num - 1)
                tt(step[j.buf][:, :], soft[:, :], lost[:, :], ALU.add).then_inc(step_done, 1)

            def product(b, n):
                pool.wait_ge(scans, N * b.num + n + 1)
                pool.wait_ge(c_loaded[n % C_RING], 16 * ((N // C_RING) * b.num + n // C_RING + 1))
                tt(state[n % H_RING][:, :], state[n % H_RING][:, :], c_all[n % C_RING][:, :], ALU.mult
                   ).then_inc(products, 1)

            def hid_norm(j):
                pool.wait_ge(hinv_done, j.num + 1)
                at_least(pool, osum_done, j.num)
                h8 = hid[:, :, :].rearrange("p d (k c) -> p (d k) c", c=C)
                tt(hnorm[:, :, :], h8, hinv[:, :].unsqueeze(2).broadcast_to([128, DIRS * CHUNKS, C]), ALU.mult
                   ).then_inc(hnorm_done, 1)

            def out_average(j):
                pool.wait_ge(osum_done, j.num + 1)
                at_least(pool, ocen_done, j.num)
                tt(oavg[:, :, :], osum[:, :, :], wf4_rows[:, :].unsqueeze(1).broadcast_to([128, CHUNKS, C]), ALU.mult
                   ).then_inc(oavg_done, 1)

            def out_square(j):
                pool.wait_ge(ocen_done, j.num + 1)
                at_least(pool, ovar_done, j.num)
                tt(osq[:, :, :], ocen[:, :, :], ocen[:, :, :], ALU.mult).then_inc(osq_done, 1)

            def out_norm(j):
                pool.wait_ge(oinv_done, j.num + 1)
                tt(onorm[:, :, :], ocen[:, :, :], oinv[:, :].unsqueeze(2).broadcast_to([128, CHUNKS, C]), ALU.mult
                   ).then_inc(onorm_done, 1)
                pool.wait_ge(onorm_done, j.num + 1)
                tt(oscaled[:, :, :], onorm[:, :, :], ln_w_rows[:, :].unsqueeze(1).broadcast_to([128, CHUNKS, C]),
                   ALU.mult).then_inc(oscaled_done, 1)
                pool.wait_ge(oscaled_done, j.num + 1)
                at_least(pool, stored, 16 * j.num)
                tt(ofin[:, :, :], oscaled[:, :, :], ln_b_rows[:, :].unsqueeze(1).broadcast_to([128, CHUNKS, C]),
                   ALU.add).then_inc(ofin_done, 1)

            def attend(j):
                return []

            def project(j):
                return [lambda g=g: g(j) for g in (soft_sum, soft_add)]

            def finish(j):
                return [lambda g=g: g(j) for g in (hid_norm, out_average, out_square, out_norm)]

            def steps(b, done, coming, later):
                for n in range(N):
                    product(b, n)
                    if n == 2 and done:
                        hid_norm(done)
                    if n == 4 and done:
                        out_average(done)
                    if n == 9 and coming:
                        soft_sum(coming)
                    if n == 10 and done:
                        out_square(done)
                    if n == 10 and coming:
                        soft_add(coming)
                    if n == 13 and done:
                        out_norm(done)

            program(pool, setup, attend, project, steps, finish)

        @block.vector
        def _(dve):
            v = nc.vector

            def setup():
                v.memset(mean_w[:, :], 1.0 / C).then_inc(zeroed, 1)
                v.memset(eps[:, :], EPS).then_inc(zeroed, 1)
                v.memset(one[:, :], 1.0).then_inc(zeroed, 1)
                v.memset(w_qkv[:, :], 0.0).then_inc(gaps_zeroed, 1)
                v.memset(w_gate[C:, :], 0.0).then_inc(zeroed, 1)
                dve.wait_ge(weights_in, 16 * N_LOADS)
                v.tensor_tensor(sigma_b[:, :], sigma[:, :], b_o2[:, :], ALU.mult)
                for tap2 in range(2):
                    v.scalar_tensor_tensor(w_conv[:, tap2, :], w_in2[:, 0:I], rms1[:, :], tap_rows[:, tap2, :],
                                           ALU.mult, ALU.mult)
                v.tensor_scalar(w_gate[0:C, :], w_in2[0:C, I:2 * I], rms1[0:C, :], None, ALU.mult)
                v.tensor_scalar(diag_d[:, :], ident[:, :], d_skip[:, :], None, ALU.mult)
                v.tensor_scalar(wf4_rows[:, :], wf_rows[:, :], 1.0 / DIRS, None, ALU.mult)
                v.tensor_scalar(neg_ident[:, :], ident[:, :], -1.0, None, ALU.mult)
                v.tensor_copy(pick_b[:, :, :], onehot[:, :].unsqueeze(2).broadcast_to([SPLIT_ROWS, N, 128]))
                dve.wait_ge(a_exp_done, 1)
                v.tensor_scalar(a_neg[:, :], a_exp[:, :], -1.0, None, ALU.mult)
                dve.wait_ge(step_w_done, 1)
                dve.wait_ge(zeroed, A_RING + 5)
                v.tensor_copy(w_step[:, :], w0[:, 0:I]).then_inc(weights_ready, 1)
                dve.wait_ge(weights_ready, 1)

            def pool2x2(dst, src):
                v.tensor_reduce(dst.rearrange("p (h w) -> p h w", h=SIDE // 2),
                                src.rearrange("p (hh dh ww dw) -> p hh ww dh dw", hh=SIDE // 2, dh=2, dw=2),
                                AX.XY, ALU.max)

            def pooling(j):
                dve.wait_ge(qkv_done, j.num + 1)
                at_least(dve, scores_done, j.num)
                pool2x2(phi_p[:, :], w0[PHI:PHI + KEY, 0:L])
                pool2x2(g_p[:, :], w0[G:G + VAL, 0:L])
                v.tensor_copy(theta[:, :], w0[THETA:THETA + KEY, 0:L]).then_inc(pooled_done, 1)

            def row_max(j):
                dve.wait_ge(scores_done, j.num + 1)
                at_least(dve, o_done, j.num)
                v.tensor_copy(gw[:, :], w0[0:POOLED, 2 * C:4 * C]).then_inc(gw_done, 1)
                at_least(dve, esc_done, j.num)
                v.tensor_reduce(nmax[:, :], w0[:, 0:CHUNKS * POOLED].rearrange("p (k m) -> p k m", k=CHUNKS), AX.X,
                                ALU.max, negate=True).then_inc(nmax_done, 1)

            def attn_norm(j):
                dve.wait_ge(esc_done, j.num + 1)
                v.reciprocal(erec[:, :], esum[:, :]).then_inc(erec_done, 1)
                dve.wait_ge(erec_done, j.num + 1)
                at_least(dve, attn_t_ps, j.num)
                v.tensor_tensor(attn[:, :, :], esc[:, :, :], erec[:, :].unsqueeze(2).broadcast_to([128, CHUNKS, POOLED]),
                                ALU.mult).then_inc(attn_done, 1)

            def residual(j):
                dve.wait_ge(o_done, j.num + 1)
                dve.wait_ge(xb_done, j.num + 1)
                at_least(dve, x2l_ps, j.num - 1)
                v.scalar_tensor_tensor(x2[j.buf][:, :], w0[:, L:2 * L], sigma[:, :], xb[:, :], ALU.mult, ALU.add
                                       ).then_inc(x2_done, 1)

            def rms(j):
                dve.wait_ge(rinv1_done, j.num + 1)
                dve.wait_ge(x2_done, j.num + 1)
                at_least(dve, gate_mm, j.num - 1)
                at_least(dve, padded, 2 * DIRS * (j.num - 1))
                v.tensor_tensor(xn[j.buf][:, :], x2[j.buf][:, :], rinv1[:, :], ALU.mult).then_inc(xn_done, 1)

            def soft_rest(j):
                dve.wait_ge(onex_done, j.num + 1)
                at_least(dve, step_done, j.num)
                v.scalar_tensor_tensor(lost[:, :], onex[:, :], 1.0, expx[:, :], ALU.subtract, ALU.subtract, reverse1=True
                                       ).then_inc(rest_done, 1)

            def scan_weight(j):
                dve.wait_ge(step_done, j.num + 1)
                dve.wait_ge(u_done, 2 * (j.num + 1))
                at_least(dve, input_done, N * (j.num - 1))
                v.tensor_tensor(du[j.buf][:, :], step[j.buf][:, :], u[j.buf][:, :], ALU.mult).then_inc(du_done, 1)

            def x2_copy(j):
                dve.wait_ge(x2l_ps, j.num + 1)
                at_least(dve, hid_done, j.num - 1)
                v.tensor_copy(x2l[j.buf][:, :], w1[:, 0:CHUNKS * C]).then_inc(x2l_done, 1)

            def scan(b, n):
                if n == 0:
                    dve.wait_ge(du_done, b.num + 1)
                dve.wait_ge(b_all_done, N * b.num + n + 1)
                v.tensor_tensor(ps_b[n % 2][:, :], du[b.buf][:, :], ps_b[n % 2][:, :], ALU.mult
                                ).then_inc(input_done, 1)
                dve.wait_ge(input_done, N * b.num + n + 1)
                dve.wait_ge(decay_done, N * b.num + n + 1)
                at_least(dve, sums, N * b.num + n - H_RING + 1)
                v.tensor_tensor_scan(state[n % H_RING][:, :], decay[n % A_RING][:, :, :].rearrange("p d t -> p (d t)"),
                                     ps_b[n % 2][:, :], 0.0, ALU.mult, ALU.add).then_inc(scans, 1)

            def gated(j):
                dve.wait_ge(sums, N * (j.num + 1))
                dve.wait_ge(gate_done, j.num + 1)
                at_least(dve, out_mm, j.num)
                for d in range(DIRS):
                    v.tensor_tensor(grid(yg[:, d, :]), ordered(ps_y[:, L * d:L * (d + 1)], d), grid(gate[j.buf][:, :]),
                                    ALU.mult).then_inc(yg_done, 1)

            def hidden(j):
                dve.wait_ge(out_mm, j.num + 1)
                dve.wait_ge(x2l_done, j.num + 1)
                at_least(dve, hnorm_done, j.num)
                v.tensor_tensor(hid[:, :, :], w1.rearrange("p (d x) -> p d x", d=DIRS),
                                x2l[j.buf][:, :].unsqueeze(1).broadcast_to([128, DIRS, CHUNKS * C]), ALU.add
                                ).then_inc(hid_done, 1)

            def dir_sum(j):
                dve.wait_ge(hnorm_done, j.num + 1)
                at_least(dve, oavg_done, j.num)
                v.tensor_reduce(osum[:, :, :].rearrange("p k c -> p (k c)"),
                                hnorm[:, :, :].rearrange("p (d k) c -> p (k c) d", d=DIRS), AX.X, ALU.add
                                ).then_inc(osum_done, 1)

            def centre(j):
                dve.wait_ge(oavg_done, j.num + 1)
                v.tensor_reduce(omean[:, :], oavg[:, :, :], AX.X, ALU.add).then_inc(omean_done, 1)
                dve.wait_ge(omean_done, j.num + 1)
                at_least(dve, onorm_done, j.num)
                v.scalar_tensor_tensor(ocen[:, :, :], omean[:, :].unsqueeze(2).broadcast_to([128, CHUNKS, C]), -1.0 / C,
                                       oavg[:, :, :], ALU.mult, ALU.add).then_inc(ocen_done, 1)

            def variance(j):
                dve.wait_ge(osq_done, j.num + 1)
                at_least(dve, oln_done, j.num)
                v.tensor_reduce(ovar[:, :], osq[:, :, :], AX.X, ALU.add).then_inc(ovar_done, 1)

            def attend(j):
                return [lambda g=g: g(j) for g in (pooling, row_max, attn_norm, residual)]

            def project(j):
                return [lambda g=g: g(j) for g in (rms, x2_copy, soft_rest,
                                                   scan_weight)]

            def finish(j):
                return [lambda g=g: g(j) for g in (gated, hidden, dir_sum, centre, variance)]

            def steps(b, done, coming, later):
                for n in range(N):
                    scan(b, n)
                    if n == 0 and coming:
                        rms(coming)
                    if n == 1 and done:
                        gated(done)
                    if n == 2 and done:
                        hidden(done)
                    if n == 3 and coming:
                        x2_copy(coming)
                    if n == 5 and done:
                        dir_sum(done)
                    if n == 10 and done:
                        centre(done)
                    if n == 11 and coming:
                        soft_rest(coming)
                    if n == 12 and done:
                        variance(done)
                    if n == 12 and later:
                        pooling(later)
                    if n == 13 and later:
                        row_max(later)
                    if n == 14 and later:
                        attn_norm(later)
                    if n == 14 and coming:
                        scan_weight(coming)
                    if n == 15 and later:
                        residual(later)

            program(dve, setup, attend, project, steps, finish)


def kernel(x, L0_conv_w_theta, L0_conv_w_phi, L0_conv_w_g, L0_conv_w_o, L0_conv_b_o, L0_conv_sigma, L1_conv_W_in,
           L1_conv_conv_w, L1_conv_conv_b, L1_conv_W_x, L1_conv_W_dt, L1_conv_b_dt, L1_conv_A_log, L1_conv_Dp,
           L1_conv_W_out, L1_conv_rms_w1, L1_conv_rms_wf, L1_conv_ln_w, L1_conv_ln_b):
    import numpy as np
    import concourse.bacc as bacc
    from concourse.bass_utils import run_bass_kernel_spmd

    x = np.asarray(x)
    arrays = {
        "x_t": x.reshape(IMAGES, L, C).transpose(0, 2, 1),
        "w_theta": L0_conv_w_theta, "w_phi": L0_conv_w_phi, "w_g": L0_conv_w_g, "w_o": L0_conv_w_o,
        "b_o": L0_conv_b_o, "sigma": np.asarray(L0_conv_sigma).reshape(1),
        "w_in_t": np.asarray(L1_conv_W_in).T, "conv_w_t": np.asarray(L1_conv_conv_w).reshape(I, TAPS).T,
        "conv_b": L1_conv_conv_b, "W_x": L1_conv_W_x, "w_x_t": np.asarray(L1_conv_W_x).T,
        "w_dt_t": np.asarray(L1_conv_W_dt).T, "b_dt": L1_conv_b_dt, "A_log": L1_conv_A_log, "Dp": L1_conv_Dp,
        "w_out_t": np.asarray(L1_conv_W_out).T, "rms_w1": L1_conv_rms_w1, "rms_wf": L1_conv_rms_wf,
        "ln_w": L1_conv_ln_w, "ln_b": L1_conv_ln_b,
        "ident": np.eye(128, dtype=np.float32),
        "onehot": np.tile(np.eye(32, N, dtype=np.float32), (COPIES, 1)),
    }
    arrays = {name: np.ascontiguousarray(v) for name, v in arrays.items()}
    nc = bacc.Bacc("TRN2", target_bir_lowering=False, num_devices=1)
    aps = {name: nc.dram_tensor(f"in_{name}", v.shape, mybir.dt.from_np(v.dtype), kind="ExternalInput").ap()
           for name, v in arrays.items()}
    out = nc.dram_tensor("out", (IMAGES, L, C), F32, kind="ExternalOutput").ap()
    build(nc, aps, out)
    r = run_bass_kernel_spmd(nc, [{f"in_{name}": v for name, v in arrays.items()}], core_ids=[0])
    return r.results[0]["out"].reshape(IMAGES, SIDE, SIDE, C)
```

```python
import concourse.bass as bass
from concourse import mybir
from contextlib import ExitStack

F32 = mybir.dt.float32
BF16 = mybir.dt.bfloat16
ALU = mybir.AluOpType
ACT = mybir.ActivationFunctionType
AX = mybir.AxisListType

IMAGES, SIDE, C = 16, 16, 64
L = SIDE * SIDE
POOLED = L // 4
KEY, VAL = C // 8, C // 2
I = 2 * C
N = 16
R = 16
TAPS = 4
DIRS = 4
T = DIRS * L
HALF = T // 2
CHUNKS = L // 128
PADDED = L + 4
EPS = 1e-5
COPIES = 3
SPLIT_ROWS = 32 * COPIES
C_ROW = SPLIT_ROWS
A_RING, H_RING, C_RING = 4, 8, 4
SUM_BEFORE = {3: (0,), 4: (1,), 6: (3,), 13: (10,)}
SUM_AFTER = {4: (2,), 7: (4,), 9: (5,), 10: (6, 7), 11: (8,), 12: (9,), 13: (11,), 15: (12,)}
SUM_NEXT = {0: (13,), 1: (14, 15)}
EXP_LN, SILU = "natural_log_exp_and_others", "silu_and_others"
THETA, PHI, G = 0, 32, 64


class Image:

    def __init__(self, pair, offset):
        self.pair, self.offset = pair, offset
        self.num = 2 * pair + offset
        self.buf = offset % 2

    def __add__(self, d):
        return Image(self.pair, self.offset + d)


def at_least(eng, sem, value):
    if not isinstance(value, int) or value > 0:
        eng.wait_ge(sem, value)


def all_at_least(eng, *waits):
    values = [v if isinstance(v, int) else eng.snap(eng.to_reg(v)) for _, v in waits]
    for (sem, _), value in zip(waits, values):
        at_least(eng, sem, value)


def build(nc, a, out):
    ctx = ExitStack()
    with ctx:
        def sb(name, shape, dt=F32):
            return ctx.enter_context(nc.sbuf_tensor(name, shape, dt))

        def ps(name, shape):
            return ctx.enter_context(nc.psum_tensor(name, shape, F32))

        def sem(name):
            return ctx.enter_context(nc.semaphore(name))

        ident = sb("ident", [128, 128])
        w_qkv = sb("w_qkv", [2 * C, 128])
        w_o2 = sb("w_o2", [VAL, 2 * C])
        sigma = sb("sigma", [128, 1])
        b_o2 = sb("b_o2", [128, 1])
        sigma_b = sb("sigma_b", [128, 1])
        w_in2 = sb("w_in2", [128, 2 * I])
        rms1 = sb("rms1", [128, 1])
        tap_rows = sb("tap_rows", [128, 2, I])
        w_conv = sb("w_conv", [128, 2, I])
        w_gate = sb("w_gate", [2 * C, I])
        conv_b = sb("conv_b", [I, 1])
        b_dt = sb("b_dt", [I, 1])
        d_skip = sb("d_skip", [I, 1])
        diag_d = sb("diag_d", [I, I])
        a_log = sb("a_log", [I, N])
        a_exp = sb("a_exp", [I, N])
        a_neg = sb("a_neg", [I, N])
        w_bc = sb("w_bc", [I, C_ROW + N])
        w_x_dt = sb("w_x_dt", [R, I])
        w_dt = sb("w_dt", [R, I])
        w_step = sb("w_step", [I, I])
        w_out = sb("w_out", [I, C])
        wf_rows = sb("wf_rows", [128, C])
        wf4_rows = sb("wf4_rows", [128, C])
        ln_w_rows = sb("ln_w_rows", [128, C])
        ln_b_rows = sb("ln_b_rows", [128, C])
        mean_w = sb("mean_w", [C, 128])
        eps = sb("eps", [128, 1])
        one = sb("one", [128, 1])
        onehot = sb("onehot", [SPLIT_ROWS, N])
        neg_ident = sb("neg_ident", [128, 128], BF16)
        pick_b = sb("pick_b", [SPLIT_ROWS, N, 128], BF16)

        xt = sb("xt", [128, L])
        xb = sb("xb", [128, L])
        theta = sb("theta", [KEY, L])
        phi_p = sb("phi_p", [KEY, POOLED])
        g_p = sb("g_p", [VAL, POOLED])
        gw = sb("gw", [POOLED, 2 * C])
        nmax = sb("nmax", [128, CHUNKS])
        esc = sb("esc", [128, CHUNKS, POOLED])
        esum = sb("esum", [128, CHUNKS])
        erec = sb("erec", [128, CHUNKS])
        attn = sb("attn", [128, CHUNKS, POOLED])
        attn_t = sb("attn_t", [POOLED, L])
        x2 = [sb(f"x2_{q}", [128, L]) for q in range(2)]
        x2sq = sb("x2sq", [C, L])
        ln1 = sb("ln1", [128, L])
        rinv1 = sb("rinv1", [128, L])
        xn = [sb(f"xn_{q}", [128, L]) for q in range(2)]
        xpad = sb("xpad", [128, DIRS, PADDED])
        u = [sb(f"u_{q}", [I, T]) for q in range(2)]
        gate = [sb(f"gate_{q}", [I, L]) for q in range(2)]
        x2l = [sb(f"x2l_{q}", [128, CHUNKS * C]) for q in range(2)]
        absx = sb("absx", [I, T])
        relx = sb("relx", [I, T])
        expx = sb("expx", [I, T])
        onex = sb("onex", [I, T])
        lnx = sb("lnx", [I, T])
        lost = sb("lost", [I, T])
        soft = sb("soft", [I, T])
        step = [sb(f"step_{q}", [I, T]) for q in range(2)]
        du = [sb(f"du_{q}", [I, T]) for q in range(2)]
        b_parts = [sb(f"b_parts_{q}", [SPLIT_ROWS, T], BF16) for q in range(2)]
        c_rows = sb("c_rows", [128, T])
        decay = [sb(f"decay_{r}", [I, DIRS, L]) for r in range(A_RING)]
        state = [sb(f"state_{r}", [I, T]) for r in range(H_RING)]
        c_all = [sb(f"c_all_{r}", [I, T]) for r in range(C_RING)]
        yg = sb("yg", [I, DIRS, L])
        hid = sb("hid", [128, DIRS, CHUNKS * C])
        hidsq = sb("hidsq", [128, DIRS * CHUNKS, C])
        hsum = sb("hsum", [128, DIRS * CHUNKS])
        hln = sb("hln", [128, DIRS * CHUNKS])
        hinv = sb("hinv", [128, DIRS * CHUNKS])
        hnorm = sb("hnorm", [128, DIRS * CHUNKS, C])
        osum = sb("osum", [128, CHUNKS, C])
        oavg = sb("oavg", [128, CHUNKS, C])
        oavg_copy = sb("oavg_copy", [128, CHUNKS, C])
        omean = sb("omean", [128, CHUNKS])
        ocen = sb("ocen", [128, CHUNKS, C])
        osq = sb("osq", [128, CHUNKS, C])
        ovar = sb("ovar", [128, CHUNKS])
        oln = sb("oln", [128, CHUNKS])
        oinv = sb("oinv", [128, CHUNKS])
        onorm = sb("onorm", [128, CHUNKS, C])
        oscaled = sb("oscaled", [128, CHUNKS, C])
        ofin = sb("ofin", [128, CHUNKS, C])

        ps_b = [ps(f"ps_b{q}", [128, T]) for q in range(2)]
        ps_y = ps("ps_y", [128, T])
        ps_w = ps("ps_w", [128, T])
        w0, w1 = ps_w[:, 0:HALF], ps_w[:, HALF:T]

        c_dram = [nc.dram_tensor(f"c_dram_{q}", [N, T], F32, kind="Internal").ap() for q in range(2)]

        qkv_weights_in = sem("qkv_weights_in")
        attn_weights_in = sem("attn_weights_in")
        attn_weights_ready = sem("attn_weights_ready")
        conv_weights_in = sem("conv_weights_in")
        conv_weights_ready = sem("conv_weights_ready")
        weights_in = sem("weights_in")
        zeroed = sem("zeroed")
        gaps_zeroed = sem("gaps_zeroed")
        a_exp_done = sem("a_exp_done")
        step_w_done = sem("step_w_done")
        weights_ready = sem("weights_ready")
        x_loaded = sem("x_loaded")
        xb_done = sem("xb_done")
        qkv_done = sem("qkv_done")
        theta_done = sem("theta_done")
        pooled_done = sem("pooled_done")
        scores_done = sem("scores_done")
        nmax_done = sem("nmax_done")
        gw_done = sem("gw_done")
        esc_done = sem("esc_done")
        erec_done = sem("erec_done")
        attn_done = sem("attn_done")
        attn_t_ps = sem("attn_t_ps")
        attn_t_done = sem("attn_t_done")
        o_done = sem("o_done")
        x2_done = sem("x2_done")
        x2sq_done = sem("x2sq_done")
        ms_done = sem("ms_done")
        ln1_done = sem("ln1_done")
        rinv1_done = sem("rinv1_done")
        xn_done = sem("xn_done")
        padded = sem("padded")
        conv_done = sem("conv_done")
        u_done = sem("u_done")
        gate_mm = sem("gate_mm")
        gate_done = sem("gate_done")
        step_mm = sem("step_mm")
        absx_done = sem("absx_done")
        relx_done = sem("relx_done")
        expx_done = sem("expx_done")
        lnx_done = sem("lnx_done")
        onex_done = sem("onex_done")
        rest_done = sem("rest_done")
        soft_done = sem("soft_done")
        step_done = sem("step_done")
        du_done = sem("du_done")
        bc_mm = sem("bc_mm")
        hi_done = sem("hi_done")
        c_rows_done = sem("c_rows_done")
        rest1_mm = sem("rest1_mm")
        rest2_mm = sem("rest2_mm")
        mid_done = sem("mid_done")
        lo_done = sem("lo_done")
        c_stored = sem("c_stored")
        x2l_ps = sem("x2l_ps")
        x2l_done = sem("x2l_done")
        decay_done = sem("decay_done")
        b_all_done = sem("b_all_done")
        input_done = sem("input_done")
        scans = sem("scans")
        c_loaded = [sem(f"c_loaded{r}") for r in range(C_RING)]
        products = sem("products")
        sums = sem("sums")
        yg_done = sem("yg_done")
        out_mm = sem("out_mm")
        hid_done = sem("hid_done")
        hsum_done = sem("hsum_done")
        hln_done = sem("hln_done")
        hinv_done = sem("hinv_done")
        hnorm_done = sem("hnorm_done")
        osum_done = sem("osum_done")
        oavg_done = sem("oavg_done")
        omean_done = sem("omean_done")
        ocen_done = sem("ocen_done")
        ovar_done = sem("ovar_done")
        oln_done = sem("oln_done")
        oinv_done = sem("oinv_done")
        onorm_done = sem("onorm_done")
        oscaled_done = sem("oscaled_done")
        ofin_done = sem("ofin_done")
        stored = sem("stored")

        def ordered(view, d):
            v = view.rearrange("p (h w) -> p h w", h=SIDE)
            if d in (2, 3):
                v = v[:, ::-1, :]
            if d in (1, 3):
                v = v[:, :, ::-1]
            return v

        def grid(view):
            return view.rearrange("p (h w) -> p h w", h=SIDE)

        column = lambda v: v.rearrange("(p a) -> p a", a=1)
        qkv_loads = [
            (w_qkv[0:C, THETA:THETA + KEY], a["w_theta"]),
            (w_qkv[0:C, PHI:PHI + KEY], a["w_phi"]),
            (w_qkv[0:C, G:G + VAL], a["w_g"]),
        ]
        attn_loads = [
            (ident[:, :], a["ident"]),
            (sigma[:, :], a["sigma"].partition_broadcast(128)),
            (b_o2[0:C, :], column(a["b_o"])),
            (b_o2[C:, :], column(a["b_o"])),
            (w_o2[:, 0:C], a["w_o"]),
            (w_o2[:, C:], a["w_o"]),
        ]
        conv_loads = [
            (w_in2[0:C, :], a["w_in_t"]),
            (w_in2[C:, :], a["w_in_t"]),
            (rms1[0:C, :], column(a["rms_w1"])),
            (rms1[C:, :], column(a["rms_w1"])),
            (tap_rows[0:C, 0, :], a["conv_w_t"][0, :].partition_broadcast(C)),
            (tap_rows[C:, 0, :], a["conv_w_t"][1, :].partition_broadcast(C)),
            (tap_rows[0:C, 1, :], a["conv_w_t"][2, :].partition_broadcast(C)),
            (tap_rows[C:, 1, :], a["conv_w_t"][3, :].partition_broadcast(C)),
            (conv_b[:, :], column(a["conv_b"])),
        ]
        loads = [
            (b_dt[:, :], column(a["b_dt"])),
            (d_skip[:, :], column(a["Dp"])),
            (a_log[:, :], a["A_log"]),
            (w_x_dt[:, :], a["W_x"][0:R, :]),
            (w_dt[:, :], a["w_dt_t"]),
            (w_out[:, :], a["w_out_t"]),
            (wf_rows[:, :], a["rms_wf"].partition_broadcast(128)),
            (ln_w_rows[:, :], a["ln_w"].partition_broadcast(128)),
            (ln_b_rows[:, :], a["ln_b"].partition_broadcast(128)),
            (onehot[:, :], a["onehot"]),
            (w_bc[:, C_ROW:C_ROW + N], a["w_x_t"][:, R + N:]),
        ]
        loads += [(w_bc[:, 32 * k:32 * k + N], a["w_x_t"][:, R:R + N]) for k in range(COPIES)]

        block = ctx.enter_context(nc.Block())

        first, last = Image(0, 0), Image(0, IMAGES - 1)

        def attn_bank(j):
            return ps_b[1][:, 0:HALF] if j.offset == 1 else w0

        def program(eng, prologue, steps, finish):
            prologue()
            steps(first, None, first + 1, first + 2)
            steps(first + 1, first, first + 2, first + 3)
            with eng.Fori(0, (IMAGES - 4) // 2) as pair:
                for offset in (2, 3):
                    b = Image(pair, offset)
                    steps(b, b + -1, b + 1, b + 2)
            steps(last + -1, last + -2, last, None)
            steps(last, last + -1, None, None)
            finish(last)

        @block.sync
        def _(sp):
            def load_weights():
                for half in range(2):
                    sp.dma_start(xt[C * half:C * half + C, :], a["x_t"][0, :, :]).then_inc(x_loaded, 16)
                sp.wait_ge(gaps_zeroed, 2)
                for dst, src in qkv_loads:
                    sp.dma_start(dst, src).then_inc(qkv_weights_in, 16)
                for dst, src in attn_loads:
                    sp.dma_start(dst, src).then_inc(attn_weights_in, 16)
                for dst, src in conv_loads:
                    sp.dma_start(dst, src).then_inc(conv_weights_in, 16)
                for dst, src in loads:
                    sp.dma_start(dst, src).then_inc(weights_in, 16)

            def load_x(j):
                all_at_least(sp, (xb_done, j.num), (qkv_done, j.num))
                sp.wait_ge(weights_ready, 1)
                for half in range(2):
                    sp.dma_start(xt[C * half:C * half + C, :], a["x_t"][j.num, :, :]).then_inc(x_loaded, 16)

            def store_c(j):
                all_at_least(sp, (c_rows_done, j.num + 1), (products, N * (j.num - 1)))
                sp.dma_start(c_dram[j.buf], c_rows[C_ROW:C_ROW + N, :]).then_inc(c_stored, 16)

            def load_c(b, n):
                stored_c = [(c_stored, 16 * (b.num + 1))] if n == 0 else []
                all_at_least(sp, *stored_c, (products, N * b.num + n - C_RING + 1))
                sp.dma_start(c_all[n % C_RING][:, :], c_dram[b.buf][n, :].partition_broadcast(128)
                             ).then_inc(c_loaded[n % C_RING], 16)

            def store_out(j):
                sp.wait_ge(ofin_done, j.num + 1)
                sp.wait_ge(weights_ready, 1)
                sp.dma_start(out[j.num, :, :].rearrange("(k p) c -> p k c", p=128), ofin[:, :, :]
                             ).then_inc(stored, 16)

            def prologue():
                load_weights()
                load_x(first + 1)
                store_c(first)

            def finish(j):
                store_out(j)

            def steps(b, done, coming, later):
                for n in range(N):
                    load_c(b, n)
                    if n == 8 and later:
                        load_x(later)
                    if n == 15 and coming:
                        store_c(coming)
                    if n == 15 and done:
                        store_out(done)

            program(sp, prologue, steps, finish)
            sp.wait_ge(stored, 16 * IMAGES)

        @block.tensor
        def _(pe):
            mm = nc.tensor.matmul

            def step_weights():
                pe.wait_ge(weights_in, 16 * len(loads))
                mm(ps_y[:, 0:I], w_x_dt[:, :], w_dt[:, :], start=True, stop=True).then_inc(step_w_done, 1)
                pe.wait_ge(weights_ready, 1)

            def qkv(j):
                pe.wait_ge(x_loaded, 32 * (j.num + 1))
                if j.offset != 1:
                    at_least(pe, lo_done, j.num)
                mm(attn_bank(j)[:, 0:L], w_qkv[:, :], xt[:, :], start=True, stop=True).then_inc(qkv_done, 1)

            def scores(j):
                pe.wait_ge(theta_done, j.num + 1)
                pe.wait_ge(pooled_done, j.num + 1)
                for k in range(CHUNKS):
                    mm(attn_bank(j)[:, POOLED * k:POOLED * (k + 1)], theta[:, 128 * k:128 * (k + 1)], phi_p[:, :],
                       start=True, stop=True)
                mm(attn_bank(j)[0:POOLED, 2 * C:4 * C], g_p[:, :], w_o2[:, :], start=True, stop=True
                   ).then_inc(scores_done, 1)

            def attn_turn(j):
                pe.wait_ge(attn_done, j.num + 1)
                pe.wait_ge(gw_done, j.num + 1)
                for k in range(CHUNKS):
                    last = mm(attn_bank(j)[0:POOLED, 128 * k:128 * (k + 1)], attn[:, k, :], ident[:, :],
                              start=True, stop=True)
                last.then_inc(attn_t_ps, 1)

            def attn_out(j):
                pe.wait_ge(attn_t_done, j.num + 1)
                mm(attn_bank(j)[:, L:2 * L], gw[:, :], attn_t[:, :], start=True, stop=True).then_inc(o_done, 1)

            def x2_turn(j):
                pe.wait_ge(x2_done, j.num + 1)
                at_least(pe, hid_done, j.num - 1)
                for k in range(CHUNKS):
                    last = mm(w1[:, C * k:C * (k + 1)], x2[j.buf][0:C, 128 * k:128 * (k + 1)], ident[0:C, 0:C],
                              start=True, stop=True)
                last.then_inc(x2l_ps, 1)

            def mean_square(j):
                pe.wait_ge(x2sq_done, j.num + 1)
                at_least(pe, lo_done, j.num)
                mm(w0[:, 0:L], mean_w[:, :], x2sq[:, :], start=True, stop=True).then_inc(ms_done, 1)

            def conv(j, half, tap2):
                if tap2 == 0:
                    pe.wait_ge(padded, 2 * DIRS * j.num + DIRS * (half + 1))
                    if half == 1:
                        pe.wait_ge(x2l_done, j.num + 1)
                mm(ps_w[:, HALF * half:HALF * (half + 1)], w_conv[:, tap2, :],
                   xpad[:, 2 * half:2 * half + 2, 2 * tap2:2 * tap2 + L],
                   start=(tap2 == 0), stop=(tap2 == 1)).then_inc(conv_done, 1)

            def gate_proj(j):
                pe.wait_ge(u_done, 2 * j.num + 1)
                mm(w0[:, 0:L], w_gate[:, :], xn[j.buf][:, :], start=True, stop=True).then_inc(gate_mm, 1)

            def step_proj(j, half):
                pe.wait_ge(u_done, 2 * (j.num + 1))
                if half == 0:
                    pe.wait_ge(gate_done, j.num + 1)
                mm(ps_w[:, HALF * half:HALF * (half + 1)], w_step[:, :],
                   u[j.buf][:, HALF * half:HALF * (half + 1)], start=True, stop=True).then_inc(step_mm, 1)

            def bc_proj(j, half):
                pe.wait_ge(relx_done, j.num + 1)
                mm(ps_w[0:C_ROW + N, HALF * half:HALF * (half + 1)], w_bc[:, :],
                   u[j.buf][:, HALF * half:HALF * (half + 1)], start=True, stop=True).then_inc(bc_mm, 1)

            def b_rest(j, level):
                rows = 32 * (COPIES - level)
                pe.wait_ge(hi_done if level == 1 else mid_done, j.num + 1)
                for half in range(2):
                    last = mm(ps_w[0:rows, HALF * half:HALF * (half + 1)], neg_ident[0:SPLIT_ROWS, 0:rows],
                              b_parts[j.buf][:, HALF * half:HALF * (half + 1)], start=False, stop=True,
                              skip_group_check=True)
                last.then_inc(rest1_mm if level == 1 else rest2_mm, 1)

            def out_proj(j, half):
                pe.wait_ge(yg_done, DIRS * j.num + 2 * (half + 1))
                if half == 0:
                    if j.offset < IMAGES - 1:
                        pe.wait_ge(lo_done, j.num + 2)
                    at_least(pe, hid_done, j.num)
                for d in (2 * half, 2 * half + 1):
                    for k in range(CHUNKS):
                        m = CHUNKS * d + k
                        last = mm(w1[:, C * m:C * (m + 1)], yg[:, d, 128 * k:128 * (k + 1)], w_out[:, :],
                                  start=True, stop=True)
                last.then_inc(out_mm, 1)

            def spread_b(b, n):
                if n == 0:
                    pe.wait_ge(lo_done, b.num + 1)
                at_least(pe, scans, N * b.num + n - 1)
                if b.offset == 0 and n == 1:
                    pe.wait_ge(x2_done, 2)
                for half in range(2):
                    last = mm(ps_b[n % 2][:, HALF * half:HALF * (half + 1)], pick_b[:, n, :],
                              b_parts[b.buf][:, HALF * half:HALF * (half + 1)], start=True, stop=True)
                last.then_inc(b_all_done, 1)

            def skip(b, half):
                mm(ps_y[:, HALF * half:HALF * (half + 1)], diag_d[:, :],
                   u[b.buf][:, HALF * half:HALF * (half + 1)], start=False, stop=False)

            def sum_state(b, n):
                pe.wait_ge(products, N * b.num + n + 1)
                if n == 0:
                    at_least(pe, yg_done, DIRS * b.num)
                for half in range(2):
                    last = mm(ps_y[:, HALF * half:HALF * (half + 1)], ident[:, :],
                              state[n % H_RING][:, HALF * half:HALF * (half + 1)],
                              start=(n == 0), stop=(n == N - 1))
                last.then_inc(sums, 1)

            def prologue():
                second = first + 1
                pe.wait_ge(qkv_weights_in, 16 * len(qkv_loads))
                qkv(first)
                pe.wait_ge(attn_weights_ready, 1)
                scores(first)
                attn_turn(first)
                attn_out(first)
                mean_square(first)
                x2_turn(first)
                pe.wait_ge(conv_weights_ready, 1)
                conv(first, 0, 0)
                conv(first, 0, 1)
                conv(first, 1, 0)
                conv(first, 1, 1)
                step_weights()
                gate_proj(first)
                step_proj(first, 1)
                step_proj(first, 0)
                qkv(second)
                scores(second)
                bc_proj(first, 0)
                bc_proj(first, 1)
                attn_turn(second)
                attn_out(second)
                b_rest(first, 1)
                b_rest(first, 2)
                spread_b(first, 0)

            def finish(j):
                for n in (0, 1):
                    for k in SUM_NEXT[n]:
                        sum_state(j, k)
                out_proj(j, 0)
                out_proj(j, 1)

            def steps(b, done, coming, later):
                for n in range(N):
                    if done:
                        for k in SUM_NEXT.get(n, ()):
                            sum_state(done, k)
                    for k in SUM_BEFORE.get(n, ()):
                        sum_state(b, k)
                    if n == 0 and coming:
                        mean_square(coming)
                    if n == 1 and coming:
                        conv(coming, 0, 0)
                        conv(coming, 0, 1)
                    if n == 2 and done:
                        out_proj(done, 0)
                        out_proj(done, 1)
                    if n == 3 and coming:
                        x2_turn(coming)
                    if n == 5 and coming:
                        conv(coming, 1, 1)
                    if n == 7 and coming:
                        step_proj(coming, 0)
                    if n == 9 and coming:
                        bc_proj(coming, 0)
                        bc_proj(coming, 1)
                    if n == 10 and coming:
                        b_rest(coming, 1)
                    if n == 10:
                        skip(b, 0)
                    if n == 11 and coming:
                        b_rest(coming, 2)
                    if n == 12 and later:
                        qkv(later)

                    if n < N - 1:
                        spread_b(b, n + 1)

                    for k in SUM_AFTER.get(n, ()):
                        sum_state(b, k)
                    if n == 4 and coming:
                        conv(coming, 1, 0)
                    if n == 5 and coming:
                        gate_proj(coming)
                    if n == 6 and coming:
                        step_proj(coming, 1)
                    if n == 7:
                        skip(b, 1)
                    if n == 12 and later:
                        scores(later)
                    if n == 14 and later:
                        attn_turn(later)
                    if n == 15 and later:
                        attn_out(later)
                    if n == 15 and coming:
                        spread_b(coming, 0)

            program(pe, prologue, steps, finish)

        @block.scalar
        def _(act):
            f = nc.scalar.activation

            def state_decay():
                act.wait_ge(weights_in, 16 * len(loads))
                f(a_exp[:, :], a_log[:, :], ACT.Exp).then_inc(a_exp_done, 1)

            def add_bias(j):
                act.wait_ge(x_loaded, 32 * (j.num + 1))
                at_least(act, x2_done, j.num)
                f(xb[:, :], xt[:, :], ACT.Identity, bias=sigma_b[:, :]).then_inc(xb_done, 1)

            def theta_copy(j):
                act.wait_ge(qkv_done, j.num + 1)
                at_least(act, scores_done, j.num)
                f(theta[:, :], attn_bank(j)[THETA:THETA + KEY, 0:L], ACT.Copy).then_inc(theta_done, 1)

            def softmax_exp(j):
                act.wait_ge(nmax_done, j.num + 1)
                at_least(act, o_done, j.num)
                f(gw[:, :], attn_bank(j)[0:POOLED, 2 * C:4 * C], ACT.Copy).then_inc(gw_done, 1)
                at_least(act, attn_done, j.num)
                for k in range(CHUNKS):
                    last = f(esc[:, k, :], attn_bank(j)[:, POOLED * k:POOLED * (k + 1)], ACT.Exp, bias=nmax[:, k:k + 1],
                             accum_out=esum[:, k:k + 1])
                last.then_inc(esc_done, 1)

            def attn_copy(j):
                act.wait_ge(attn_t_ps, j.num + 1)
                at_least(act, o_done, j.num)
                f(attn_t[:, :], attn_bank(j)[0:POOLED, 0:L], ACT.Copy).then_inc(attn_t_done, 1)

            def square(j):
                act.wait_ge(x2_done, j.num + 1)
                at_least(act, ms_done, j.num)
                f(x2sq[:, :], x2[j.buf][0:C, :], ACT.Square).then_inc(x2sq_done, 1)

            def rms_inverse(j):
                act.wait_ge(ms_done, j.num + 1)
                f(ln1[:, :], w0[:, 0:L], ACT.Ln, bias=eps[:, :]).then_inc(ln1_done, 1)
                at_least(act, xn_done, j.num)
                act.wait_ge(ln1_done, j.num + 1)
                f(rinv1[:, :], ln1[:, :], ACT.Exp, scale=-0.5).then_inc(rinv1_done, 1)

            def pad(j, half):
                act.wait_ge(xn_done, j.num + 1)
                at_least(act, conv_done, 4 * j.num)
                for d in (2 * half, 2 * half + 1):
                    f(grid(xpad[0:C, d, 3:3 + L]), ordered(xn[j.buf][0:C, :], d), ACT.Copy).then_inc(padded, 1)
                    f(grid(xpad[C:, d, 2:2 + L]), ordered(xn[j.buf][C:, :], d), ACT.Copy).then_inc(padded, 1)

            def conv_silu(j):
                act.preload_act_table_set(SILU)
                act.wait_ge(conv_done, 4 * j.num + 2)
                at_least(act, sums, N * (j.num - 1))
                at_least(act, du_done, j.num - 1)
                f(u[j.buf][:, 0:HALF], w0, ACT.Silu, bias=conv_b[:, :]).then_inc(u_done, 1)
                act.wait_ge(conv_done, 4 * (j.num + 1))
                f(u[j.buf][:, HALF:T], w1, ACT.Silu, bias=conv_b[:, :]).then_inc(u_done, 1)

            def gate_silu(j):
                act.wait_ge(gate_mm, j.num + 1)
                at_least(act, yg_done, DIRS * (j.num - 1))
                f(gate[j.buf][:, :], w0[:, 0:L], ACT.Silu).then_inc(gate_done, 1)
                act.preload_act_table_set(EXP_LN)

            def softplus_in(j):
                act.wait_ge(step_mm, 2 * (j.num + 1))
                f(absx[:, :], ps_w[:, :], ACT.Abs, bias=b_dt[:, :]).then_inc(absx_done, 1)
                at_least(act, soft_done, j.num)
                f(relx[:, :], ps_w[:, :], ACT.Relu, bias=b_dt[:, :]).then_inc(relx_done, 1)

            def softplus_exp(j):
                act.wait_ge(absx_done, j.num + 1)
                at_least(act, rest_done, j.num)
                f(expx[:, :], absx[:, :], ACT.Exp, scale=-1.0).then_inc(expx_done, 1)
                act.wait_ge(expx_done, j.num + 1)
                f(onex[:, :], expx[:, :], ACT.Identity, bias=one[:, :]).then_inc(onex_done, 1)

            def softplus_ln(j):
                act.wait_ge(onex_done, j.num + 1)
                f(lnx[:, :], onex[:, :], ACT.Ln).then_inc(lnx_done, 1)

            def b_hi(j):
                act.wait_ge(bc_mm, 2 * (j.num + 1))
                at_least(act, b_all_done, N * (j.num - 1))
                f(b_parts[j.buf][:, :], ps_w[0:SPLIT_ROWS, :], ACT.Copy).then_inc(hi_done, 1)

            def c_copy(j):
                act.wait_ge(bc_mm, 2 * (j.num + 1))
                at_least(act, c_stored, 16 * j.num)
                f(c_rows[C_ROW:C_ROW + N, :], ps_w[C_ROW:C_ROW + N, :], ACT.Copy).then_inc(c_rows_done, 1)

            def b_mid(j):
                act.wait_ge(rest1_mm, j.num + 1)
                f(b_parts[j.buf][0:64, :], ps_w[0:64, :], ACT.Copy).then_inc(mid_done, 1)

            def b_lo(j):
                act.wait_ge(rest2_mm, j.num + 1)
                f(b_parts[j.buf][0:32, :], ps_w[0:32, :], ACT.Copy).then_inc(lo_done, 1)

            def decays(b, n):
                if n == 0:
                    act.wait_ge(step_done, b.num + 1)
                at_least(act, scans, N * b.num + n - A_RING + 1)
                f(decay[n % A_RING][:, :, 1:L], step[b.buf][:, :].rearrange("p (d t) -> p d t", d=DIRS)[:, :, 1:L],
                  ACT.Exp, scale=a_neg[:, n:n + 1]).then_inc(decay_done, 1)

            def hid_inverse(j):
                act.wait_ge(hid_done, j.num + 1)
                at_least(act, hln_done, j.num)
                for d in range(DIRS):
                    for k in range(CHUNKS):
                        m = CHUNKS * d + k
                        last = f(hidsq[:, m, :], hid[:, d, C * k:C * (k + 1)], ACT.Square, accum_out=hsum[:, m:m + 1])
                last.then_inc(hsum_done, 1)
                act.wait_ge(hsum_done, j.num + 1)
                f(hln[:, :], hsum[:, :], ACT.Ln, bias=eps[:, :], scale=1.0 / C).then_inc(hln_done, 1)
                act.wait_ge(hln_done, j.num + 1)
                at_least(act, hnorm_done, j.num)
                f(hinv[:, :], hln[:, :], ACT.Exp, scale=-0.5).then_inc(hinv_done, 1)

            def out_mean(j):
                act.wait_ge(oavg_done, j.num + 1)
                at_least(act, ocen_done, j.num)
                for k in range(CHUNKS):
                    last = f(oavg_copy[:, k, :], oavg[:, k, :], ACT.Identity, accum_out=omean[:, k:k + 1])
                last.then_inc(omean_done, 1)

            def out_inverse(j):
                act.wait_ge(ocen_done, j.num + 1)
                at_least(act, oln_done, j.num)
                for k in range(CHUNKS):
                    last = f(osq[:, k, :], ocen[:, k, :], ACT.Square, accum_out=ovar[:, k:k + 1])
                last.then_inc(ovar_done, 1)
                act.wait_ge(ovar_done, j.num + 1)
                f(oln[:, :], ovar[:, :], ACT.Ln, bias=eps[:, :], scale=1.0 / C).then_inc(oln_done, 1)
                act.wait_ge(oln_done, j.num + 1)
                at_least(act, onorm_done, j.num)
                f(oinv[:, :], oln[:, :], ACT.Exp, scale=-0.5).then_inc(oinv_done, 1)

            def prologue():
                second = first + 1
                act.preload_act_table_set(EXP_LN)
                theta_copy(first)
                act.wait_ge(attn_weights_ready, 1)
                add_bias(first)
                softmax_exp(first)
                attn_copy(first)
                square(first)
                rms_inverse(first)
                act.wait_ge(zeroed, A_RING + 5)
                pad(first, 0)
                pad(first, 1)
                state_decay()
                conv_silu(first)
                gate_silu(first)
                act.wait_ge(weights_ready, 1)
                softplus_in(first)
                theta_copy(second)
                softplus_exp(first)
                add_bias(second)
                softmax_exp(second)
                b_hi(first)
                softplus_ln(first)
                attn_copy(second)
                b_mid(first)
                square(second)
                c_copy(first)
                b_lo(first)

            def finish(j):
                hid_inverse(j)
                out_mean(j)
                out_inverse(j)

            def steps(b, done, coming, later):
                for n in range(N):
                    decays(b, n)
                    if not done and coming:
                        if n == 0:
                            rms_inverse(coming)
                        if n == 1:
                            pad(coming, 0)
                            pad(coming, 1)
                    elif coming:
                        if n == 0:
                            add_bias(coming)
                            softmax_exp(coming)
                        if n == 1:
                            attn_copy(coming)
                            square(coming)
                        if n == 2:
                            rms_inverse(coming)
                        if n == 3:
                            pad(coming, 0)
                            pad(coming, 1)
                    if n == 5 and done:
                        hid_inverse(done)
                    if n == 7 and coming:
                        conv_silu(coming)
                        gate_silu(coming)
                    if n == 8 and coming:
                        softplus_in(coming)
                    if n == 9 and coming:
                        softplus_exp(coming)
                        b_hi(coming)
                        softplus_ln(coming)
                    if n == 11 and done:
                        out_mean(done)
                    if n == 11 and coming:
                        b_mid(coming)
                        c_copy(coming)
                    if n == 12 and coming:
                        b_lo(coming)
                    if n == 14 and later:
                        theta_copy(later)
                    if n == 15 and done:
                        out_inverse(done)

            program(act, prologue, steps, finish)

        @block.gpsimd
        def _(pool):
            tt = nc.gpsimd.tensor_tensor

            def setup():
                nc.gpsimd.memset(w_bc[:, :], 0.0).then_inc(gaps_zeroed, 1)
                nc.gpsimd.memset(xpad[:, :, :], 0.0).then_inc(zeroed, 1)
                for r in range(A_RING):
                    nc.gpsimd.memset(decay[r][:, :, 0:1], 0.0).then_inc(zeroed, 1)
                pool.wait_ge(weights_ready, 1)

            def soft_sum(j):
                pool.wait_ge(lnx_done, j.num + 1)
                pool.wait_ge(relx_done, j.num + 1)
                at_least(pool, step_done, j.num)
                tt(soft[:, :], lnx[:, :], relx[:, :], ALU.add).then_inc(soft_done, 1)

            def soft_add(j):
                pool.wait_ge(soft_done, j.num + 1)
                pool.wait_ge(rest_done, j.num + 1)
                at_least(pool, decay_done, N * (j.num - 1))
                at_least(pool, du_done, j.num - 1)
                tt(step[j.buf][:, :], soft[:, :], lost[:, :], ALU.add).then_inc(step_done, 1)

            def product(b, n):
                pool.wait_ge(scans, N * b.num + n + 1)
                pool.wait_ge(c_loaded[n % C_RING], 16 * ((N // C_RING) * b.num + n // C_RING + 1))
                tt(state[n % H_RING][:, :], state[n % H_RING][:, :], c_all[n % C_RING][:, :], ALU.mult
                   ).then_inc(products, 1)

            def hid_norm(j):
                pool.wait_ge(hinv_done, j.num + 1)
                at_least(pool, osum_done, j.num)
                h8 = hid[:, :, :].rearrange("p d (k c) -> p (d k) c", c=C)
                tt(hnorm[:, :, :], h8, hinv[:, :].unsqueeze(2).broadcast_to([128, DIRS * CHUNKS, C]), ALU.mult
                   ).then_inc(hnorm_done, 1)

            def out_average(j):
                pool.wait_ge(osum_done, j.num + 1)
                at_least(pool, ocen_done, j.num)
                tt(oavg[:, :, :], osum[:, :, :], wf4_rows[:, :].unsqueeze(1).broadcast_to([128, CHUNKS, C]), ALU.mult
                   ).then_inc(oavg_done, 1)

            def out_norm(j):
                pool.wait_ge(oinv_done, j.num + 1)
                tt(onorm[:, :, :], ocen[:, :, :], oinv[:, :].unsqueeze(2).broadcast_to([128, CHUNKS, C]), ALU.mult
                   ).then_inc(onorm_done, 1)
                pool.wait_ge(onorm_done, j.num + 1)
                tt(oscaled[:, :, :], onorm[:, :, :], ln_w_rows[:, :].unsqueeze(1).broadcast_to([128, CHUNKS, C]),
                   ALU.mult).then_inc(oscaled_done, 1)
                pool.wait_ge(oscaled_done, j.num + 1)
                at_least(pool, stored, 16 * j.num)
                tt(ofin[:, :, :], oscaled[:, :, :], ln_b_rows[:, :].unsqueeze(1).broadcast_to([128, CHUNKS, C]),
                   ALU.add).then_inc(ofin_done, 1)

            def prologue():
                setup()
                soft_sum(first)
                soft_add(first)

            def finish(j):
                hid_norm(j)
                out_average(j)
                out_norm(j)

            def steps(b, done, coming, later):
                for n in range(N):
                    product(b, n)
                    if n == 6 and done:
                        hid_norm(done)
                    if n == 8 and done:
                        out_average(done)
                    if n == 9 and coming:
                        soft_sum(coming)
                        soft_add(coming)
                    if n == 12 and done:
                        out_norm(done)

            program(pool, prologue, steps, finish)

        @block.vector
        def _(dve):
            v = nc.vector

            def constants():
                v.memset(w_qkv[:, :], 0.0).then_inc(gaps_zeroed, 1)
                v.memset(mean_w[:, :], 1.0 / C).then_inc(zeroed, 1)
                v.memset(eps[:, :], EPS).then_inc(zeroed, 1)
                v.memset(one[:, :], 1.0).then_inc(zeroed, 1)
                v.memset(w_gate[C:, :], 0.0).then_inc(zeroed, 1)

            def attn_setup():
                dve.wait_ge(attn_weights_in, 16 * len(attn_loads))
                v.tensor_tensor(sigma_b[:, :], sigma[:, :], b_o2[:, :], ALU.mult).then_inc(attn_weights_ready, 1)

            def conv_setup():
                dve.wait_ge(conv_weights_in, 16 * len(conv_loads))
                for tap2 in range(2):
                    v.scalar_tensor_tensor(w_conv[:, tap2, :], w_in2[:, 0:I], rms1[:, :], tap_rows[:, tap2, :],
                                           ALU.mult, ALU.mult)
                v.tensor_scalar(w_gate[0:C, :], w_in2[0:C, I:2 * I], rms1[0:C, :], None, ALU.mult
                                ).then_inc(conv_weights_ready, 1)

            def setup():
                dve.wait_ge(weights_in, 16 * len(loads))
                v.tensor_scalar(diag_d[:, :], ident[:, :], d_skip[:, :], None, ALU.mult)
                v.tensor_scalar(wf4_rows[:, :], wf_rows[:, :], 1.0 / DIRS, None, ALU.mult)
                v.tensor_scalar(neg_ident[:, :], ident[:, :], -1.0, None, ALU.mult)
                v.tensor_copy(pick_b[:, :, :], onehot[:, :].unsqueeze(2).broadcast_to([SPLIT_ROWS, N, 128]))
                dve.wait_ge(a_exp_done, 1)
                v.tensor_scalar(a_neg[:, :], a_exp[:, :], -1.0, None, ALU.mult)
                dve.wait_ge(step_w_done, 1)
                dve.wait_ge(zeroed, A_RING + 5)
                v.tensor_copy(w_step[:, :], ps_y[:, 0:I]).then_inc(weights_ready, 1)
                dve.wait_ge(weights_ready, 1)

            def pool2x2(dst, src):
                return v.tensor_reduce(dst.rearrange("p (h w) -> p h w", h=SIDE // 2),
                                       src.rearrange("p (hh dh ww dw) -> p hh ww dh dw", hh=SIDE // 2, dh=2, dw=2),
                                       AX.XY, ALU.max)

            def pooling(j):
                dve.wait_ge(qkv_done, j.num + 1)
                at_least(dve, scores_done, j.num)
                pool2x2(phi_p[:, :], attn_bank(j)[PHI:PHI + KEY, 0:L])
                pool2x2(g_p[:, :], attn_bank(j)[G:G + VAL, 0:L]).then_inc(pooled_done, 1)

            def row_max(j):
                dve.wait_ge(scores_done, j.num + 1)
                at_least(dve, esc_done, j.num)
                v.tensor_reduce(nmax[:, :],
                                attn_bank(j)[:, 0:CHUNKS * POOLED].rearrange("p (k m) -> p k m", k=CHUNKS),
                                AX.X, ALU.max, negate=True).then_inc(nmax_done, 1)

            def attn_norm(j):
                dve.wait_ge(esc_done, j.num + 1)
                v.reciprocal(erec[:, :], esum[:, :]).then_inc(erec_done, 1)
                dve.wait_ge(erec_done, j.num + 1)
                at_least(dve, attn_t_ps, j.num)
                v.tensor_tensor(attn[:, :, :], esc[:, :, :],
                                erec[:, :].unsqueeze(2).broadcast_to([128, CHUNKS, POOLED]), ALU.mult
                                ).then_inc(attn_done, 1)

            def residual(j):
                dve.wait_ge(o_done, j.num + 1)
                dve.wait_ge(xb_done, j.num + 1)
                at_least(dve, x2l_ps, j.num - 1)
                v.scalar_tensor_tensor(x2[j.buf][:, :], attn_bank(j)[:, L:2 * L], sigma[:, :], xb[:, :],
                                       ALU.mult, ALU.add).then_inc(x2_done, 1)

            def rms(j):
                dve.wait_ge(rinv1_done, j.num + 1)
                dve.wait_ge(x2_done, j.num + 1)
                at_least(dve, gate_mm, j.num - 1)
                at_least(dve, padded, 2 * DIRS * (j.num - 1))
                v.tensor_tensor(xn[j.buf][:, :], x2[j.buf][:, :], rinv1[:, :], ALU.mult).then_inc(xn_done, 1)

            def soft_rest(j):
                dve.wait_ge(onex_done, j.num + 1)
                at_least(dve, step_done, j.num)
                v.scalar_tensor_tensor(lost[:, :], onex[:, :], 1.0, expx[:, :], ALU.subtract, ALU.subtract,
                                       reverse1=True).then_inc(rest_done, 1)

            def scan_weight(j):
                dve.wait_ge(step_done, j.num + 1)
                dve.wait_ge(u_done, 2 * (j.num + 1))
                at_least(dve, input_done, N * (j.num - 1))
                v.tensor_tensor(du[j.buf][:, :], step[j.buf][:, :], u[j.buf][:, :], ALU.mult).then_inc(du_done, 1)

            def x2_copy(j):
                dve.wait_ge(x2l_ps, j.num + 1)
                at_least(dve, hid_done, j.num - 1)
                v.tensor_copy(x2l[j.buf][:, :], w1[:, 0:CHUNKS * C]).then_inc(x2l_done, 1)

            def scan_input(b, n):
                if n == 0:
                    dve.wait_ge(du_done, b.num + 1)
                dve.wait_ge(b_all_done, N * b.num + n + 1)
                v.tensor_tensor(ps_b[n % 2][:, :], du[b.buf][:, :], ps_b[n % 2][:, :], ALU.mult
                                ).then_inc(input_done, 1)

            def scan(b, n):
                dve.wait_ge(input_done, N * b.num + n + 1)
                dve.wait_ge(decay_done, N * b.num + n + 1)
                at_least(dve, sums, N * b.num + n - H_RING + 1)
                v.tensor_tensor_scan(state[n % H_RING][:, :], decay[n % A_RING][:, :, :].rearrange("p d t -> p (d t)"),
                                     ps_b[n % 2][:, :], 0.0, ALU.mult, ALU.add).then_inc(scans, 1)

            def gated(j):
                dve.wait_ge(sums, N * (j.num + 1))
                dve.wait_ge(gate_done, j.num + 1)
                at_least(dve, out_mm, 2 * j.num)
                for d in range(DIRS):
                    v.tensor_tensor(grid(yg[:, d, :]), ordered(ps_y[:, L * d:L * (d + 1)], d), grid(gate[j.buf][:, :]),
                                    ALU.mult).then_inc(yg_done, 1)

            def hidden(j):
                dve.wait_ge(out_mm, 2 * (j.num + 1))
                dve.wait_ge(x2l_done, j.num + 1)
                at_least(dve, hnorm_done, j.num)
                v.tensor_tensor(hid[:, :, :], w1.rearrange("p (d x) -> p d x", d=DIRS),
                                x2l[j.buf][:, :].unsqueeze(1).broadcast_to([128, DIRS, CHUNKS * C]), ALU.add
                                ).then_inc(hid_done, 1)

            def dir_sum(j):
                dve.wait_ge(hnorm_done, j.num + 1)
                at_least(dve, oavg_done, j.num)
                v.tensor_reduce(osum[:, :, :].rearrange("p k c -> p (k c)"),
                                hnorm[:, :, :].rearrange("p (d k) c -> p (k c) d", d=DIRS), AX.X, ALU.add
                                ).then_inc(osum_done, 1)

            def centre(j):
                dve.wait_ge(omean_done, j.num + 1)
                at_least(dve, onorm_done, j.num)
                v.scalar_tensor_tensor(ocen[:, :, :], omean[:, :].unsqueeze(2).broadcast_to([128, CHUNKS, C]), -1.0 / C,
                                       oavg[:, :, :], ALU.mult, ALU.add).then_inc(ocen_done, 1)

            def prologue():
                second = first + 1
                constants()
                pooling(first)
                attn_setup()
                row_max(first)
                attn_norm(first)
                residual(first)
                rms(first)
                x2_copy(first)
                conv_setup()
                setup()
                pooling(second)
                row_max(second)
                attn_norm(second)
                soft_rest(first)
                residual(second)
                scan_weight(first)

            def finish(j):
                gated(j)
                hidden(j)
                dir_sum(j)
                centre(j)

            def steps(b, done, coming, later):
                for n in range(N):
                    scan_input(b, n)
                    if n == 0 and coming:
                        rms(coming)
                    if n == 1 and done:
                        gated(done)
                    if n == 2 and done:
                        hidden(done)
                    if n == 4 and coming:
                        x2_copy(coming)
                    if n == 9 and done:
                        dir_sum(done)
                    if n == 10 and coming:
                        soft_rest(coming)
                    if n == 11 and done:
                        centre(done)
                    if n == 12 and later:
                        pooling(later)
                    if n == 13 and later:
                        row_max(later)
                    if n == 14 and later:
                        attn_norm(later)
                    if n == 15 and later:
                        residual(later)

                    scan(b, n)
                    if n == 15 and coming:
                        scan_weight(coming)

            program(dve, prologue, steps, finish)


def kernel(x, L0_conv_w_theta, L0_conv_w_phi, L0_conv_w_g, L0_conv_w_o, L0_conv_b_o, L0_conv_sigma, L1_conv_W_in,
           L1_conv_conv_w, L1_conv_conv_b, L1_conv_W_x, L1_conv_W_dt, L1_conv_b_dt, L1_conv_A_log, L1_conv_Dp,
           L1_conv_W_out, L1_conv_rms_w1, L1_conv_rms_wf, L1_conv_ln_w, L1_conv_ln_b):
    import numpy as np
    import concourse.bacc as bacc
    from concourse.bass_utils import run_bass_kernel_spmd

    x = np.asarray(x)
    arrays = {
        "x_t": x.reshape(IMAGES, L, C).transpose(0, 2, 1),
        "w_theta": L0_conv_w_theta, "w_phi": L0_conv_w_phi, "w_g": L0_conv_w_g, "w_o": L0_conv_w_o,
        "b_o": L0_conv_b_o, "sigma": np.asarray(L0_conv_sigma).reshape(1),
        "w_in_t": np.asarray(L1_conv_W_in).T, "conv_w_t": np.asarray(L1_conv_conv_w).reshape(I, TAPS).T,
        "conv_b": L1_conv_conv_b, "W_x": L1_conv_W_x, "w_x_t": np.asarray(L1_conv_W_x).T,
        "w_dt_t": np.asarray(L1_conv_W_dt).T, "b_dt": L1_conv_b_dt, "A_log": L1_conv_A_log, "Dp": L1_conv_Dp,
        "w_out_t": np.asarray(L1_conv_W_out).T, "rms_w1": L1_conv_rms_w1, "rms_wf": L1_conv_rms_wf,
        "ln_w": L1_conv_ln_w, "ln_b": L1_conv_ln_b,
        "ident": np.eye(128, dtype=np.float32),
        "onehot": np.tile(np.eye(32, N, dtype=np.float32), (COPIES, 1)),
    }
    arrays = {name: np.ascontiguousarray(v) for name, v in arrays.items()}
    nc = bacc.Bacc("TRN2", target_bir_lowering=False, num_devices=1)
    aps = {name: nc.dram_tensor(f"in_{name}", v.shape, mybir.dt.from_np(v.dtype), kind="ExternalInput").ap()
           for name, v in arrays.items()}
    out = nc.dram_tensor("out", (IMAGES, L, C), F32, kind="ExternalOutput").ap()
    build(nc, aps, out)
    r = run_bass_kernel_spmd(nc, [{f"in_{name}": v for name, v in arrays.items()}], core_ids=[0])
    return r.results[0]["out"].reshape(IMAGES, SIDE, SIDE, C)
```
